# Optimizing a Trainium2 kernel written in Bass

```python
import numpy as np
import jax
import jax.numpy as jnp

def _softmax(x, axis=-1):
    return jax.nn.softmax(x, axis=axis)

def _gelu(x):
    return jax.nn.gelu(x, approximate=True)

def _silu(x):
    return jax.nn.silu(x)

def _sigmoid(x):
    return jax.nn.sigmoid(x)

def _layernorm(x, axis=-1, eps=1e-05):
    m = jnp.mean(x, axis=axis, keepdims=True)
    v = jnp.var(x, axis=axis, keepdims=True)
    return (x - m) / jnp.sqrt(v + eps)

def _scatter_add(tgt, idx, src, axis=0):
    return tgt.at[idx].add(src)

def _segment_sum(src, seg, n):
    return jax.ops.segment_sum(src, seg, n)
kernel_name = 'mk_adaln_d1_jaxref_r8_efa4a6'

def setup_inputs(seed: int=0):
    np.random.seed(seed)
    _w = jnp.asarray

    def _L0_attn_setup():
        import jax, jax.numpy as jnp
        import numpy as np
        HEADS = 16
        DIM_HEAD = 128
        SCALE = 16.0
        EPS = 1e-05

        def _layernorm(x, g):
            mu = jnp.mean(x, axis=-1, keepdims=True)
            var = jnp.mean((x - mu) ** 2, axis=-1, keepdims=True)
            return (x - mu) * jax.lax.rsqrt(var + EPS) * g

        def _l2norm(t):
            return t * jax.lax.rsqrt(jnp.sum(t * t, axis=-1, keepdims=True) + 1e-12)
        key = jax.random.key(seed)
        ks = jax.random.split(key, 5)
        B, N, dim = (2, 256, 256)
        hidden = HEADS * DIM_HEAD
        x = jax.random.normal(ks[0], (B, N, dim), dtype=jnp.float32)
        g_norm = jnp.ones((dim,), dtype=jnp.float32)
        Wq = jax.random.normal(ks[1], (dim, hidden), dtype=jnp.float32) * dim ** (-0.5)
        Wkv = jax.random.normal(ks[2], (dim, 2 * DIM_HEAD), dtype=jnp.float32) * dim ** (-0.5)
        Wout = jax.random.normal(ks[3], (hidden, dim), dtype=jnp.float32) * hidden ** (-0.5)
        g_out = jnp.ones((dim,), dtype=jnp.float32)
        return {'x': x, 'g_norm': g_norm, 'Wq': Wq, 'Wkv': Wkv, 'Wout': Wout, 'g_out': g_out}
    _L0_attn_in = _L0_attn_setup()

    def _L0_ffn_setup():
        import jax, jax.numpy as jnp
        import numpy as np
        H = 256
        I = 176
        E = 8
        K = 2
        B, S = (4, 256)

        def _moe(x, router_w, w1, w2):
            b, s, h = x.shape
            xf = x.reshape(-1, h)
            T = xf.shape[0]
            logits = xf @ router_w.T
            topk_vals, topk_idx = jax.lax.top_k(logits, K)
            topk_w = jax.nn.softmax(topk_vals, axis=-1)
            exp_id = topk_idx.reshape(-1)
            exp_w = topk_w.reshape(-1)
            order = jnp.argsort(exp_id)
            x_sorted = xf[order // K]
            counts = jnp.bincount(exp_id, length=E).astype(jnp.int32)
            y1 = jax.lax.ragged_dot(x_sorted, jnp.swapaxes(w1, 1, 2), counts)
            gate, up = jnp.split(y1, 2, axis=-1)
            y_act = jax.nn.silu(gate) * up
            y2 = jax.lax.ragged_dot(y_act, jnp.swapaxes(w2, 1, 2), counts)
            inv = jnp.argsort(order)
            y_pairs = y2[inv] * exp_w[:, None]
            y = y_pairs.reshape(T, K, h).sum(axis=1)
            return y.reshape(b, s, h)
        key = jax.random.key(seed)
        k1, k2, k3, k4 = jax.random.split(key, 4)
        x = jax.random.normal(k1, (B, S, H), dtype=jnp.float32)
        router_w = jax.random.normal(k2, (E, H), dtype=jnp.float32) * 0.02
        w1 = jax.random.normal(k3, (E, 2 * I, H), dtype=jnp.float32) * 0.02
        w2 = jax.random.normal(k4, (E, H, I), dtype=jnp.float32) * 0.02
        return {'x': x, 'router_w': router_w, 'w1': w1, 'w2': w2}
    _L0_ffn_in = _L0_ffn_setup()
    _L0_c = _w((lambda *s: np.random.randn(*s).astype(np.float32) * 0.05)(2, 256))
    _L0_wmod = _w((lambda *s: np.random.randn(*s).astype(np.float32) * 0.05)(256, 6 * 256) * 256 ** (-0.5))
    _d = {'L0_attn_x': _L0_attn_in['x'], 'L0_attn_g_norm': _L0_attn_in['g_norm'], 'L0_attn_Wq': _L0_attn_in['Wq'], 'L0_attn_Wkv': _L0_attn_in['Wkv'], 'L0_attn_Wout': _L0_attn_in['Wout'], 'L0_attn_g_out': _L0_attn_in['g_out'], 'L0_ffn_router_w': _L0_ffn_in['router_w'], 'L0_ffn_w1': _L0_ffn_in['w1'], 'L0_ffn_w2': _L0_ffn_in['w2'], 'L0_c': _L0_c, 'L0_wmod': _L0_wmod}
    _x0 = _d['L0_attn_x']
    _d['L0_attn_x'] = jax.random.normal(jax.random.fold_in(jax.random.key(seed), 1), (2, 1024, 256), dtype=_x0.dtype)
    del _x0
    return _d

def reference(L0_attn_x, L0_attn_g_norm, L0_attn_Wq, L0_attn_Wkv, L0_attn_Wout, L0_attn_g_out, L0_ffn_router_w, L0_ffn_w1, L0_ffn_w2, L0_c, L0_wmod):

    def _L0_attn_ref(x, g_norm, Wq, Wkv, Wout, g_out):
        import jax, jax.numpy as jnp
        import numpy as np
        HEADS = 16
        DIM_HEAD = 128
        SCALE = 16.0
        EPS = 1e-05

        def _layernorm(x, g):
            mu = jnp.mean(x, axis=-1, keepdims=True)
            var = jnp.mean((x - mu) ** 2, axis=-1, keepdims=True)
            return (x - mu) * jax.lax.rsqrt(var + EPS) * g

        def _l2norm(t):
            return t * jax.lax.rsqrt(jnp.sum(t * t, axis=-1, keepdims=True) + 1e-12)
        B, N, dim = x.shape
        xn = _layernorm(x, g_norm)
        q = xn @ Wq
        kv = xn @ Wkv
        k, v = (kv[..., :DIM_HEAD], kv[..., DIM_HEAD:])
        q = q.reshape(B, N, HEADS, DIM_HEAD).transpose(0, 2, 1, 3)
        q = q * SCALE
        q = _l2norm(q)
        k = _l2norm(k)
        s = jnp.sqrt(SCALE).astype(x.dtype)
        q = q * s
        k = k * s
        sim = jnp.einsum('bhid,bjd->bhij', q, k)
        attn = jax.nn.softmax(sim.astype(jnp.float32), axis=-1).astype(sim.dtype)
        out = jnp.einsum('bhij,bjd->bhid', attn, v)
        out = out.transpose(0, 2, 1, 3).reshape(B, N, HEADS * DIM_HEAD)
        out = out @ Wout
        return _layernorm(out, g_out)

    def _L0_ffn_ref(x, router_w, w1, w2):
        import jax, jax.numpy as jnp
        import numpy as np
        H = 256
        I = 176
        E = 8
        K = 2
        B, S = (4, 256)

        def _moe(x, router_w, w1, w2):
            b, s, h = x.shape
            xf = x.reshape(-1, h)
            T = xf.shape[0]
            logits = xf @ router_w.T
            topk_vals, topk_idx = jax.lax.top_k(logits, K)
            topk_w = jax.nn.softmax(topk_vals, axis=-1)
            exp_id = topk_idx.reshape(-1)
            exp_w = topk_w.reshape(-1)
            order = jnp.argsort(exp_id)
            x_sorted = xf[order // K]
            counts = jnp.bincount(exp_id, length=E).astype(jnp.int32)
            y1 = jax.lax.ragged_dot(x_sorted, jnp.swapaxes(w1, 1, 2), counts)
            gate, up = jnp.split(y1, 2, axis=-1)
            y_act = jax.nn.silu(gate) * up
            y2 = jax.lax.ragged_dot(y_act, jnp.swapaxes(w2, 1, 2), counts)
            inv = jnp.argsort(order)
            y_pairs = y2[inv] * exp_w[:, None]
            y = y_pairs.reshape(T, K, h).sum(axis=1)
            return y.reshape(b, s, h)
        return _moe(x, router_w, w1, w2)
    x = L0_attn_x
    mod = (_silu(L0_c) @ L0_wmod).reshape(L0_c.shape[0], 6, 1, -1)
    sa, ca, ga, sb, cb, gb = (mod[:, 0], mod[:, 1], mod[:, 2], mod[:, 3], mod[:, 4], mod[:, 5])
    ga = (2 * (ga >= 0) - 1) * jnp.maximum(jnp.abs(ga), 0.25)
    gb = (2 * (gb >= 0) - 1) * jnp.maximum(jnp.abs(gb), 0.25)
    h = _layernorm(x, axis=-1) * (1 + ca) + sa
    x = x + ga * _L0_attn_ref(h, L0_attn_g_norm, L0_attn_Wq, L0_attn_Wkv, L0_attn_Wout, L0_attn_g_out)
    h = _layernorm(x, axis=-1) * (1 + cb) + sb
    x = x + gb * _L0_ffn_ref(h, L0_ffn_router_w, L0_ffn_w1, L0_ffn_w2)
    return x

_drawn_inputs = setup_inputs


def setup_inputs(seed=0):
    import zlib

    import numpy as np

    out = dict(_drawn_inputs(seed))
    spreads = {'L0_attn_g_norm': (1.0, 0.2), 'L0_attn_g_out': (1.0, 0.2)}
    factors = {'L0_ffn_router_w': 8.0, 'L0_ffn_w1': 8.0, 'L0_ffn_w2': 8.0}
    for name, (base, spread) in spreads.items():
        noise = np.random.default_rng([zlib.crc32(name.encode()), seed]).standard_normal(out[name].shape)
        drawn = base * np.exp(spread * noise) if base else spread * noise
        out[name] = jnp.asarray(drawn.astype(out[name].dtype))
    for name, factor in factors.items():
        out[name] = (out[name] * factor).astype(out[name].dtype)
    return out
```

```python
from contextlib import ExitStack

import numpy as np

import concourse.bass as bass
from concourse import mybir

P = 128
BANK = 512
B, N, D = 2, 1024, 256
EPS_LN = 1e-5
EPS_Q = 1e-12 / 256.0
EPS_K = 1e-12
POOL_CONSTANTS = (-0.5, 1.5, EPS_LN, EPS_K, EPS_Q)
KC = D // P
HEADS, DH = 16, 128
PAIRS = HEADS // 2
NT = N // P
CH = N // BANK
STEPS = 2 * NT
ITERS = B * PAIRS
E, TOPK, INNER = 8, 2, 176
ROWS = E * INNER
RT = ROWS // P
GROUPS = B * N // BANK
GT = BANK // P
SMALL = P + 1 + E
SHIFT, SCALE, GATE = 0, 1, 2

F32 = mybir.dt.float32
F32R = mybir.dt.float32r
U32 = mybir.dt.uint32
ALU = mybir.AluOpType
ACT = mybir.ActivationFunctionType
AX = mybir.AxisListType

HI, LO = 0, 1
PASSES = ((LO, HI), (HI, HI), (HI, LO))


def shape_constants():
    select = np.zeros((P, ROWS), np.float32)
    for k in range(2 * E):
        select[k, (k % E) * INNER:(k % E + 1) * INNER] = 1.0
    not_hi = np.zeros((P, 1), np.float32)
    not_hi[E:2 * E] = -1.0
    experts = np.tile(np.arange(E, dtype=np.float32), (P, 1))
    return np.concatenate([np.eye(P, dtype=np.float32), not_hi, experts, select], axis=1)


def adaln_block(nc, x, g_norm, wq, wkv, wout, g_out, router, w_gate, w_up, w_down, cond, wmod,
                consts, out):
    ctx = ExitStack()
    with ctx:
        def sb(name, shape, dt=F32, where=ctx):
            return where.enter_context(nc.sbuf_tensor(name, shape, dt))

        def sem(name):
            return ctx.enter_context(nc.semaphore(name))

        small = sb("small", [P, SMALL])
        ident = small[:, 0:P]
        experts = small[:, P + 1:SMALL]
        ones = sb("ones", [P, 1])
        mod = sb("mod", [P, B, 6, D])
        gout = sb("gout", [P, D])
        gate_sign = sb("gate_sign", [P, B, D])
        gnorm = sb("gnorm", [P, KC])
        condT = sb("condT", [P, KC, B])
        cond_e = sb("cond_e", [P, KC, B])
        silu_rows = sb("silu_rows", [P, KC, B, P])
        resid = sb("resid", [P, B * NT, D])
        xT = [sb(f"xT{b}", [P, 2, KC, N], F32R) for b in range(B)]
        LNS = 4 * GROUPS
        ln_stats = sb("ln_stats", [P, LNS, GT, 6])
        ln_mv = sb("ln_mv", [P, LNS, GT, 2])
        ln_r = sb("ln_r", [P, LNS, GT])
        ln_nb = sb("ln_nb", [P, LNS, GT])
        ln_t = sb("ln_t", [P, 3, GT])
        pool_c = sb("pool_c", [P, len(POOL_CONSTANTS), GT])
        z = sb("z", [P, GT, D])
        wkv_raw = sb("wkv_raw", [P, KC, 2 * DH])

        early = ExitStack()
        wmod_sb = sb("wmod_sb", [P, KC, 6 * D], where=early)
        w_raw = sb("w_raw", [P, KC, HEADS * DH], where=early)
        w_hi = sb("w_hi", [P, 2 * PAIRS, KC * D // 2], F32R, where=early)
        w_lo = sb("w_lo", [P, 2 * PAIRS, KC * D // 2], F32R, where=early)
        early.close()

        mid = ExitStack()
        p32 = sb("p32", [P, 4, N], where=mid)
        phi = sb("phi", [P, 4, N], F32R, where=mid)
        plo = sb("plo", [P, 2, N], F32R, where=mid)
        psums = sb("psums", [P, 2, N], where=mid)
        oT = sb("oT", [P, 2, N], F32R, where=mid)
        wout_sb = [sb(f"wout_sb{h}", [P, 2, D], F32R, where=mid) for h in range(2)]
        kT = [sb(f"kT{b}", [P, 2, N], F32R, where=mid) for b in range(B)]
        v = [sb(f"v{b}", [P, 2, NT, DH], F32R, where=mid) for b in range(B)]
        qT = sb("qT", [P, 2, 2, N], F32R, where=mid)
        qn = sb("qn", [P, NT, 2, DH], where=mid)
        q_raw = sb("q_raw", [P, 2, 2, 2, DH], where=mid)
        q_sq = sb("q_sq", [P, 2, 2, DH], where=mid)
        q_ss = sb("q_ss", [P, 4], where=mid)
        q_t = sb("q_t", [P, 3, 4], where=mid)
        q_rn = sb("q_rn", [P, 2, 4], where=mid)
        rz = sb("rz", [P, 2, NT], where=mid)
        wq_sb = sb("wq_sb", [P, 2, KC, D], F32R, where=mid)
        wkv_sb = sb("wkv_sb", [P, 2, KC, D], F32R, where=mid)
        mid.close()

        late = ExitStack()
        gu_w = sb("gu_w", [P, 2, 2, KC, ROWS], F32R, where=late)
        down_w = sb("down_w", [P, 2, RT, D], F32R, where=late)
        e_raw = sb("e_raw", [P, KC, ROWS], where=late)
        down_raw = e_raw[:, :, :].rearrange("p k n -> p (k n)").rearrange("p (r f) -> p r f", f=D)
        x_again = sb("x_again", [P, GT, D], where=late)
        logits = sb("logits", [P, GT, E], where=late)
        top = sb("top", [P, GT, 8], where=late)
        top_at = sb("top_at", [P, GT, 8], U32, where=late)
        top_f = sb("top_f", [P, GT, TOPK], where=late)
        r_d = sb("r_d", [P, GT], where=late)
        r_e = sb("r_e", [P, GT], where=late)
        r_den = sb("r_den", [P, GT], where=late)
        r_w = sb("r_w", [P, GT, TOPK], where=late)
        r_one = sb("r_one", [P, GT, E], where=late)
        r_two = sb("r_two", [P, GT, E], where=late)
        route = sb("route", [P, GT, 2 * E], where=late)
        rT_hi = sb("rT_hi", [2 * E, BANK], F32R, where=late)
        rT = sb("rT", [2 * E, B * N], F32R, where=late)
        select_raw = sb("select_raw", [2 * E, ROWS], where=late)
        select = sb("select", [2 * E, ROWS], F32R, where=late)
        router_raw = sb("router_raw", [P, KC, E], where=late)
        router_sb = sb("router_sb", [P, 2, KC, E], F32R, where=late)
        act_s = sb("act_s", [P, 2, BANK], where=late)
        act_u = sb("act_u", [P, BANK], where=late)
        act_a = sb("act_a", [P, 2, BANK], where=late)
        act_hi = sb("act_hi", [P, 2, BANK], F32R, where=late)
        act_lo = sb("act_lo", [P, 2, BANK], F32R, where=late)
        o_sb = sb("o_sb", [P, GT, D], where=late)
        late.close()

        pS = ctx.enter_context(nc.psum_tensor("pS", [P, 2, CH, BANK], F32))
        pO = ctx.enter_context(nc.psum_tensor("pO", [P, CH, BANK], F32))
        pX = ctx.enter_context(nc.psum_tensor("pX", [P, BANK], F32))
        pY = ctx.enter_context(nc.psum_tensor("pY", [P, BANK], F32))

        wq_split = nc.dram_tensor("wq_split", [ITERS, P, 2, KC * D], F32, kind="Internal").ap()
        wout_split = nc.dram_tensor("wout_split", [2 * ITERS, P, 2, D], F32, kind="Internal").ap()

        (dma_c, dma_const, dma_wmod, dma_wq, dma_wkv, dma_wout, dma_scratch, dma_out,
         wq_in, wouta_in, woutb_in, dma_w1, dma_w2, dma_w3, dma_moe) = map(sem, (
             "dma_c dma_const dma_wmod dma_wq dma_wkv dma_wout dma_scratch dma_out "
             "wq_in wouta_in woutb_in dma_w1 dma_w2 dma_w3 dma_moe").split())
        dma_x = [sem(f"dma_x{g}") for g in range(GROUPS)]
        x_again_in = sem("x_again_in")
        (cond_exp, cond_den, silu_ready, mod_ready, mod_copied, mod_done) = map(sem, (
            "cond_exp cond_den silu_ready mod_ready mod_copied mod_done").split())
        constants_made = sem("constants_made")
        (ln_sem, stats_ready, rstd_chain, rstd_ready, normed, modulated) = map(sem, (
            "ln_sem stats_ready rstd_chain rstd_ready normed modulated").split())
        (whi_ready, wlo_ready) = map(sem, "whi_ready wlo_ready".split())
        (x_job_ready, x_bank_free) = map(sem, "x_job_ready x_bank_free".split())
        (q_copied, q_ss_ready, q_chain, q_rn_ready, qn_ready, t_hi_ready, t_lo_ready) = map(sem, (
            "q_copied q_ss_ready q_chain q_rn_ready qn_ready t_hi_ready t_lo_ready").split())
        (v_hi_ready, v_lo_ready) = map(sem, "v_hi_ready v_lo_ready".split())
        (scores_ready, phi_ready, p32_ready, plo_ready, psum_added, pv_done) = map(sem, (
            "scores_ready phi_ready p32_ready plo_ready psum_added pv_done").split())
        (o_hi_ready, o_lo_ready, y_job_ready, y_bank_free) = map(sem, (
            "o_hi_ready o_lo_ready y_job_ready y_bank_free").split())
        (xt_ready, xt_hi_ready, xt_lo_ready) = map(sem, "xt_ready xt_hi_ready xt_lo_ready".split())
        (logits_ready, logits_copied, top_ready, route_chain, exp_ready, route_ready, rT_psum,
         rT_hi_ready, rT_ready) = map(sem, (
             "logits_ready logits_copied top_ready route_chain exp_ready route_ready rT_psum "
             "rT_hi_ready rT_ready").split())
        (gu_ready, cw_ready, silu_done, u_done, a_done, ahi_done, alo_done, down_done, o_mul,
         o_done, ehi_ready, elo_ready, misc_ready) = map(sem, (
             "gu_ready cw_ready silu_done u_done a_done ahi_done alo_done down_done o_mul "
             "o_done ehi_ready elo_ready misc_ready").split())

        def q_job(n, k):
            return 4 * n + k + 1

        def t_job(n, k):
            return 2 * B + 4 * n + k + 1

        def x_job(it, k):
            return 6 * B + 6 + 8 * it + k + 1

        def y_job(head, k):
            return 5 * head + k + 1

        def added(it, s):
            it, s = it + s // STEPS, s % STEPS
            return 7 * (2 * it + s // NT) + max(s % NT, 1)

        def step(it, s):
            return STEPS * it + s

        def ln_first(g):
            return 2 * g

        def ln_third(g):
            return 2 * GROUPS + 2 * g

        tokens = x.rearrange("b (t p) f -> p (b t) f", p=P)
        out_tokens = out.rearrange("b (t p) f -> p (b t) f", p=P)

        def iterations(eng, body):
            for b in range(B):
                body(PAIRS * b, b, True, False)
                with eng.Fori(PAIRS * b + 1, PAIRS * b + PAIRS - 1) as it:
                    body(it, b, False, False)
                body(PAIRS * b + PAIRS - 1, b, False, True)

        block = ctx.enter_context(nc.Block())

        @block.sync
        def _(sp):
            sp.dma_start(condT[:, :, :], cond).then_inc(dma_c, 16)
            for g in range(GROUPS):
                sp.dma_start(resid[:, GT * g:GT * g + GT, :], tokens[:, GT * g:GT * g + GT, :]).then_inc(dma_x[g], 16)
                if g == 0:
                    sp.dma_start(wmod_sb[:, :, :], wmod.rearrange("(k p) n -> p k n", p=P)).then_inc(dma_wmod, 16)
            sp.dma_start(small[:, :], consts[:, 0:SMALL]).then_inc(dma_const, 16)
            sp.dma_start(gnorm[:, :], g_norm).then_inc(dma_const, 16)
            sp.dma_start(gout[:, :], g_out.rearrange("(a f) -> a f", a=1).broadcast_to([P, D])).then_inc(dma_const, 16)

            sp.dma_start(wkv_raw[:, :, :], wkv.rearrange("(k p) n -> p k n", p=P)).then_inc(dma_wkv, 16)
            sp.dma_start(w_raw[:, :, :], wq.rearrange("(k p) n -> p k n", p=P)).then_inc(dma_wq, 16)
            sp.wait_ge(whi_ready, KC + 2)
            sp.wait_ge(wlo_ready, KC + 2)
            for b in range(B):
                for part, w in ((HI, w_hi), (LO, w_lo)):
                    dst = wq_split[PAIRS * b:PAIRS * b + PAIRS, :, part, :].rearrange("n p f -> p n f")
                    sp.dma_start(dst, w[:, :, :].rearrange("p (n a) f -> p n (a f)", a=2).bitcast(F32)).then_inc(dma_scratch, 16)
            sp.dma_start(w_raw[:, :, :].rearrange("p k (h n) -> p (k h) n", n=D),
                         wout.rearrange("(h d) n -> d h n", d=DH)).then_inc(dma_wout, 16)
            sp.wait_ge(whi_ready, KC + 3)
            sp.wait_ge(wlo_ready, KC + 3)
            for b in range(B):
                for part, w in ((HI, w_hi), (LO, w_lo)):
                    dst = wout_split[HEADS * b:HEADS * b + HEADS, :, part, :].rearrange("n p f -> p n f")
                    sp.dma_start(dst, w[:, :, :].bitcast(F32)).then_inc(dma_scratch, 16)
            sp.wait_ge(dma_scratch, 16 * 8)

            def load_wq(n):
                sp.dma_start(wq_sb[:, :, :, :].rearrange("p s k f -> p s (k f)").bitcast(F32),
                             wq_split[n, :, :, :] if isinstance(n, int) else
                             wq_split[bass.ds(n, 1), :, :, :].rearrange("n p s f -> p (n s) f")).then_inc(wq_in, 16)

            def load_wout(head, buf, landed):
                sp.dma_start(wout_sb[buf][:, :, :].bitcast(F32),
                             wout_split[head, :, :, :] if isinstance(head, int) else
                             wout_split[bass.ds(head, 1), :, :, :].rearrange("n p s f -> p (n s) f")).then_inc(landed, 16)

            load_wq(0)
            load_wout(0, 0, wouta_in)
            sp.wait_ge(q_copied, q_job(2, 3))
            load_wq(1)

            def loads(it, b, first, last):
                if not (first and b == 0):
                    sp.wait_ge(y_bank_free, y_job(2 * it - 1, 4))
                load_wout(2 * it + 1, 1, woutb_in)
                if not (b == B - 1 and last):
                    sp.wait_ge(q_copied, q_job(2 + it + 1, 3))
                    if not isinstance(it, int) or it + 2 < ITERS:
                        load_wq(it + 2)
                    sp.wait_ge(y_bank_free, y_job(2 * it, 4))
                    load_wout(2 * it + 2, 0, wouta_in)

            for b in range(B):
                loads(PAIRS * b, b, True, False)
                with sp.Fori(PAIRS * b + 1, PAIRS * b + PAIRS - 2) as it:
                    loads(it, b, False, False)
                loads(PAIRS * b + PAIRS - 2, b, False, False)
                loads(PAIRS * b + PAIRS - 1, b, False, True)

            sp.wait_ge(y_bank_free, y_job(2 * ITERS - 1, 4))
            sp.dma_start(router_raw[:, :, :], router.rearrange("(k p) e -> p k e", p=P)).then_inc(dma_moe, 16)
            sp.dma_start(select_raw[:, :], consts[0:2 * E, SMALL:SMALL + ROWS]).then_inc(dma_moe, 16)
            sp.dma_start(x_again[:, :, :], tokens[:, 0:GT, :]).then_inc(x_again_in, 16)
            sp.dma_start(e_raw[:, :, :], w_gate.rearrange("(k p) n -> p k n", p=P)).then_inc(dma_w1, 16)
            sp.wait_ge(elo_ready, 1)
            sp.dma_start(e_raw[:, :, :], w_up.rearrange("(k p) n -> p k n", p=P)).then_inc(dma_w2, 16)
            sp.wait_ge(elo_ready, 2)
            sp.dma_start(down_raw, w_down.rearrange("(r p) f -> p r f", p=P)).then_inc(dma_w3, 16)
            for g in range(1, GROUPS):
                sp.wait_ge(modulated, 2 * GROUPS + 4 * g - 2)
                sp.dma_start(x_again[:, :, :], tokens[:, GT * g:GT * g + GT, :]).then_inc(x_again_in, 16)
            for g in range(GROUPS):
                sp.wait_ge(o_done, g + 1)
                sp.dma_start(out_tokens[:, GT * g:GT * g + GT, :], o_sb[:, :, :]).then_inc(dma_out, 16)
            sp.wait_ge(dma_out, 16 * GROUPS)

        @block.gpsimd
        def _(pool):
            minus_half, three_halves, eps_ln, eps_k, eps_q = (pool_c[:, i, :] for i in range(len(POOL_CONSTANTS)))
            for i, value in enumerate(POOL_CONSTANTS):
                nc.gpsimd.memset(pool_c[:, i, :], value).then_inc(constants_made, 1)
            nc.gpsimd.memset(ones[:, :], 1.0).then_inc(constants_made, 1)
            pool.wait_ge(constants_made, len(POOL_CONSTANTS) + 1)
            def newton(value, eps, t, dst, done, count):
                steps = (
                    lambda: nc.gpsimd.tensor_tensor(t[0], value, eps, ALU.add),
                    lambda: nc.gpsimd.tensor_tensor(t[1], t[0], minus_half, ALU.pow),
                    lambda: nc.gpsimd.tensor_tensor(t[2], t[1], t[1], ALU.mult),
                    lambda: nc.gpsimd.tensor_tensor(t[2], t[2], t[0], ALU.mult),
                    lambda: nc.gpsimd.tensor_tensor(t[2], t[2], minus_half, ALU.mult),
                    lambda: nc.gpsimd.tensor_tensor(t[2], t[2], three_halves, ALU.add),
                )
                for i, make in enumerate(steps):
                    make().then_inc(done, 1)
                    pool.wait_ge(done, count + i + 1)
                return nc.gpsimd.tensor_tensor(dst, t[1], t[2], ALU.mult)

            def rstd(n):
                pool.wait_ge(stats_ready, n + 1)
                t = [ln_t[:, i, :] for i in range(3)]
                newton(ln_mv[:, n, :, 1], eps_ln, t, ln_r[:, n, :], rstd_chain, 8 * n).then_inc(rstd_chain, 1)
                pool.wait_ge(rstd_chain, 8 * n + 7)
                nc.gpsimd.tensor_tensor(t[0], ln_mv[:, n, :, 0], ln_r[:, n, :], ALU.mult).then_inc(rstd_chain, 1)
                pool.wait_ge(rstd_chain, 8 * n + 8)
                nc.gpsimd.tensor_scalar(ln_nb[:, n, :], t[0], -1.0, None, ALU.mult).then_inc(rstd_ready, 1)
                pool.wait_ge(rstd_ready, n + 1)

            def q_norm(n, k, eps):
                pool.wait_ge(q_ss_ready, q_job(n, k))
                if not (isinstance(n, int) and n == 0 and k < 2):
                    pool.wait_ge(qn_ready, q_job(n, k) - 2)
                newton(q_ss[:, :], eps, [q_t[:, i, :] for i in range(3)], q_rn[:, k % 2, :],
                       q_chain, 6 * (q_job(n, k) - 1)).then_inc(q_rn_ready, 1)
                pool.wait_ge(q_rn_ready, q_job(n, k))

            for g in range(GROUPS):
                for n in (ln_first(g), ln_first(g) + 1):
                    rstd(n)
            for n in range(B + 1):
                for k in range(4):
                    q_norm(n, k, eps_k if n < B else eps_q)

            def norms(it, b, first, last):
                if not (b == B - 1 and last):
                    for k in range(4):
                        q_norm(it + 3, k, eps_q)

            iterations(pool, norms)
            for g in range(GROUPS):
                for n in (ln_third(g), ln_third(g) + 1):
                    rstd(n)

        @block.scalar
        def _(act):
            act.wait_ge(dma_c, 16)
            nc.scalar.activation(cond_e[:, :, :], condT[:, :, :], ACT.Exp, scale=-1.0).then_inc(cond_exp, 1)
            for c in range(3):
                for b in range(B):
                    i = B * c + b
                    act.wait_ge(mod_ready, i + 1)
                    src = (pS[:, i // 2, i % 2, :] if i < 4 else pO[:, i % 2, :]).rearrange("p (a f) -> p a f", a=2)
                    nc.scalar.copy(mod[:, b, 2 * c:2 * c + 2, :], src).then_inc(mod_copied, 1)
            act.wait_ge(dma_const, 16 * 3)
            act.wait_ge(dma_wkv, 16)
            for k in range(KC):
                nc.scalar.activation(wkv_sb[:, HI, k, :], wkv_raw[:, k, :], ACT.Copy, scale=gnorm[:, k:k + 1]).then_inc(whi_ready, 1)

            def normalise(n, src):
                act.wait_ge(rstd_ready, n + 1)
                for t in range(GT):
                    nc.scalar.activation(z[:, t, :], src[:, t, :], ACT.Identity, scale=ln_r[:, n, t:t + 1],
                                         bias=ln_nb[:, n, t:t + 1]).then_inc(normed, 1)

            def transposed_hi(i, b, c):
                for k in range(KC):
                    act.wait_ge(xt_ready, KC * i + k + 1)
                    nc.scalar.copy(xT[b][:, HI, k, c * BANK:(c + 1) * BANK], pS[:, 0, k, :]).then_inc(xt_hi_ready, 1)

            for g in range(GROUPS):
                if g:
                    act.wait_ge(xt_ready, KC * g)
                normalise(ln_first(g), resid[:, GT * g:GT * g + GT, :])
                normalise(ln_first(g) + 1, z)
                transposed_hi(g, g // 2, g % 2)
                if g == 0:
                    act.wait_ge(dma_wq, 16)
                    for k in range(KC):
                        nc.scalar.activation(
                            w_hi[:, :, :].rearrange("p (n a) f -> p a n f", a=2)[:, k], w_raw[:, k, :].rearrange("p (n f) -> p n f", f=D),
                            ACT.Copy, scale=gnorm[:, k:k + 1]).then_inc(whi_ready, 1)
            act.wait_ge(dma_wout, 16)
            act.wait_ge(dma_scratch, 16 * 4)
            nc.scalar.copy(w_hi[:, :, :].rearrange("p h f -> p (h f)"), w_raw[:, :, :].rearrange("p k n -> p (k n)")).then_inc(whi_ready, 1)

            def q_copy(n, k, bank_job):
                act.wait_ge(x_job_ready, bank_job)
                if not (isinstance(n, int) and n == 0 and k < 2):
                    act.wait_ge(qn_ready, q_job(n, k) - 2)
                if isinstance(n, int) and n < B and not (n == 0 and k < 2):
                    act.wait_ge(v_lo_ready, 4 * n + k - 1)
                if isinstance(n, int) and n == B and k < 2:
                    act.wait_ge(v_lo_ready, 4 * n + k - 1)
                src = pX[:, :].rearrange("p (t h d) -> p t h d", t=2, h=2)
                nc.scalar.copy(q_raw[:, k % 2, :, :, :], src).then_inc(q_copied, 1)
                if not (isinstance(n, int) and n == 0 and k == 0):
                    act.wait_ge(q_ss_ready, q_job(n, k) - 1)
                nc.scalar.activation(q_sq[:, :, :, :], src, ACT.Square).then_inc(x_bank_free, 1)

            def t_hi(dst, bank_job):
                act.wait_ge(x_job_ready, bank_job)
                nc.scalar.copy(dst, pX[:, :]).then_inc(t_hi_ready, 1)

            def chunk(c):
                return slice(c * BANK, (c + 1) * BANK)

            for b in range(B):
                for k in range(4):
                    q_copy(b, k, 6 * b + k + 1)
                    act.wait_ge(q_copied, q_job(b, k))
                    nc.scalar.copy(v[b][:, HI, 2 * k:2 * k + 2, :], q_raw[:, k % 2, :, 1, :]).then_inc(v_hi_ready, 1)
                for c in range(CH):
                    t_hi(kT[b][:, HI, chunk(c)], 6 * b + 4 + c + 1)
            for k in range(4):
                q_copy(2, k, 6 * B + k + 1)
            for c in range(CH):
                t_hi(qT[:, 0, HI, chunk(c)], 6 * B + 4 + c + 1)

            def o_hi(head, free):
                act.wait_ge(pv_done, NT * (head + 1))
                if free:
                    act.wait_ge(y_job_ready, y_job(head - 1, 4))
                nc.scalar.copy(oT[:, HI, :].rearrange("p (c n) -> p c n", c=CH), pO[:, :, :]).then_inc(o_hi_ready, 1)

            def steps(it, b, first, last):
                start, end = b == 0 and first, b == B - 1 and last
                for s in range(STEPS):
                    t = step(it, s)
                    act.wait_ge(scores_ready, t + 1)
                    if not (start and s < 4):
                        act.wait_ge(pv_done, t - 3)
                    nc.scalar.activation(phi[:, s % 4, :].rearrange("p (c n) -> p c n", c=CH), pS[:, s % 2, :, :],
                                         ACT.Exp, scale=16.0).then_inc(phi_ready, 1)
                    if not (start and s < 4):
                        act.wait_ge(psum_added, added(it, s - 4))
                    nc.scalar.activation(p32[:, s % 4, :].rearrange("p (c n) -> p c n", c=CH), pS[:, s % 2, :, :],
                                         ACT.Exp, scale=16.0).then_inc(p32_ready, 1)
                    if s in B_AT:
                        c = B_AT.index(s)
                        t_hi(qT[:, 1, HI, chunk(c)], x_job(it, c))
                    if s in Q_AT and not end:
                        q_copy(it + 3, Q_AT.index(s), x_job(it, 2 + Q_AT.index(s)))
                    if s in A_AT and not end:
                        c = A_AT.index(s)
                        t_hi(qT[:, 0, HI, chunk(c)], x_job(it, 6 + c))
                    if s == 0 and not start:
                        o_hi(2 * it - 1, True)
                    if s == NT:
                        o_hi(2 * it, not start)

            act.wait_ge(dma_scratch, 16 * 8)
            iterations(act, steps)
            o_hi(2 * ITERS - 1, True)

            act.wait_ge(y_bank_free, y_job(2 * ITERS - 1, 4))
            act.wait_ge(dma_moe, 32)
            nc.scalar.copy(select[:, :], select_raw[:, :]).then_inc(misc_ready, 1)
            nc.scalar.copy(router_sb[:, HI, :, :], router_raw[:, :, :]).then_inc(misc_ready, 1)
            for i, landed in enumerate((dma_w1, dma_w2, dma_w3)):
                act.wait_ge(landed, 16)
                nc.scalar.copy(gu_w[:, i, HI, :, :] if i < 2 else down_w[:, HI, :, :], e_raw[:, :, :] if i < 2 else down_raw).then_inc(ehi_ready, 1)
            for g in range(GROUPS):
                if g:
                    act.wait_ge(xt_ready, KC * (GROUPS + g))
                normalise(ln_third(g), resid[:, GT * g:GT * g + GT, :])
                act.wait_ge(modulated, 2 * GROUPS + 4 * g + 2)
                normalise(ln_third(g) + 1, resid[:, GT * g:GT * g + GT, :])
                transposed_hi(GROUPS + g, g // 2, g % 2)
                act.wait_ge(top_ready, g + 1)
                nc.scalar.activation(r_e[:, :], r_d[:, :], ACT.Exp).then_inc(exp_ready, 1)
                act.wait_ge(rT_psum, g + 1)
                if g:
                    act.wait_ge(rT_ready, g)
                nc.scalar.copy(rT_hi[:, :], pX[0:2 * E, :]).then_inc(rT_hi_ready, 1)
            for g in range(GROUPS):
                for t in range(RT):
                    n = RT * g + t
                    act.wait_ge(gu_ready, n + 1)
                    if before(g, t) > 0:
                        act.wait_ge(u_done, before(g, t))
                    nc.scalar.activation(act_s[:, t % 2, :], pS[:, t % 2, 0, :], ACT.Silu).then_inc(silu_done, 1)
                    act.wait_ge(a_done, n + 1)
                    if before(g, t) > 0:
                        act.wait_ge(down_done, before(g, t))
                    nc.scalar.copy(act_hi[:, t % 2, :], act_a[:, t % 2, :]).then_inc(ahi_done, 1)

        @block.vector
        def _(dve):
            dve.wait_ge(cond_exp, 1)
            nc.vector.tensor_scalar(cond_e[:, :, :], cond_e[:, :, :], 1.0, None, ALU.add).then_inc(cond_den, 1)
            dve.wait_ge(cond_den, 1)
            nc.vector.reciprocal(cond_e[:, :, :], cond_e[:, :, :]).then_inc(cond_den, 1)
            dve.wait_ge(cond_den, 2)
            nc.vector.tensor_tensor(condT[:, :, :], condT[:, :, :], cond_e[:, :, :], ALU.mult).then_inc(cond_den, 1)
            dve.wait_ge(cond_den, 3)
            nc.vector.tensor_copy(silu_rows[:, :, :, :], condT[:, :, :].unsqueeze(3).broadcast_to([P, KC, B, P])).then_inc(silu_ready, 1)

            def ln(n, src, count=None):
                for t in range(GT):
                    ins = nc.vector.bn_stats(ln_stats[:, n, t, :], src[:, t, :])
                ins.then_inc(ln_sem, 1)
                dve.wait_ge(ln_sem, n + 1)
                for t in range(GT):
                    ins = nc.vector.bn_aggr(ln_mv[:, n, t, :], ln_stats[:, n, t, :])
                ins.then_inc(stats_ready, 1)

            def rows(b, which):
                return mod[:, b, which, :].unsqueeze(1).broadcast_to([P, GT, D])

            def transposed_lo(i, b, c):
                for k in range(KC):
                    dve.wait_ge(xt_hi_ready, KC * i + k + 1)
                    nc.vector.tensor_tensor(xT[b][:, LO, k, c * BANK:(c + 1) * BANK], pS[:, 0, k, :],
                                            xT[b][:, HI, k, c * BANK:(c + 1) * BANK], ALU.subtract).then_inc(xt_lo_ready, 1)

            def modulate(b, half_rows, count, normed_count):
                dve.wait_ge(normed, normed_count)
                nc.vector.tensor_tensor(z[:, :, :], z[:, :, :], rows(b, half_rows + SCALE), ALU.mult).then_inc(modulated, 1)
                dve.wait_ge(modulated, count)
                nc.vector.tensor_tensor(z[:, :, :], z[:, :, :], rows(b, half_rows + SHIFT), ALU.add).then_inc(modulated, 1)
                dve.wait_ge(modulated, count + 1)

            for g in range(GROUPS):
                dve.wait_ge(dma_x[g], 16)
                ln(ln_first(g), resid[:, GT * g:GT * g + GT, :])
                if g == 0:
                    dve.wait_ge(mod_copied, 2 * 3)
                    for h in (0, 3):
                        nc.vector.tensor_scalar(mod[:, :, h + SCALE, :], mod[:, :, h + SCALE, :], 1.0, None, ALU.add).then_inc(mod_done, 1)
                    dve.wait_ge(mod_done, 2)
                modulate(g // 2, 0, 2 * g + 1, 2 * GT * g + GT)
                ln(ln_first(g) + 1, z)
                transposed_lo(g, g // 2, g % 2)
                if g == 0:
                    for k in range(KC):
                        dve.wait_ge(whi_ready, k + 1)
                        nc.vector.scalar_tensor_tensor(out=wkv_sb[:, LO, k, :], in0=wkv_raw[:, k, :], scalar=gnorm[:, k:k + 1],
                                                       in1=wkv_sb[:, HI, k, :], op0=ALU.mult, op1=ALU.subtract).then_inc(wlo_ready, 1)
                    for k in range(KC):
                        dve.wait_ge(whi_ready, KC + k + 1)
                        view = [w[:, :, :].rearrange("p (n a) f -> p a n f", a=2)[:, k] for w in (w_hi, w_lo)]
                        nc.vector.scalar_tensor_tensor(out=view[LO], in0=w_raw[:, k, :].rearrange("p (n f) -> p n f", f=D),
                                                       scalar=gnorm[:, k:k + 1], in1=view[HI], op0=ALU.mult, op1=ALU.subtract).then_inc(wlo_ready, 1)
            for i, h in enumerate((GATE, 3 + GATE)):
                nc.vector.tensor_scalar(gate_sign[:, :, :], mod[:, :, h, :], 0.0, 2.0, ALU.is_ge, ALU.mult).then_inc(mod_done, 1)
                nc.vector.scalar_tensor_tensor(out=mod[:, :, h, :], in0=mod[:, :, h, :], scalar=-1.0, in1=mod[:, :, h, :],
                                               op0=ALU.mult, op1=ALU.max).then_inc(mod_done, 1)
                dve.wait_ge(mod_done, 4 * i + 4)
                nc.vector.tensor_scalar(mod[:, :, h, :], mod[:, :, h, :], 0.25, None, ALU.max).then_inc(mod_done, 1)
                dve.wait_ge(mod_done, 4 * i + 5)
                nc.vector.scalar_tensor_tensor(out=mod[:, :, h, :], in0=gate_sign[:, :, :], scalar=-1.0, in1=mod[:, :, h, :],
                                               op0=ALU.add, op1=ALU.mult).then_inc(mod_done, 1)
                dve.wait_ge(mod_done, 4 * i + 6)
            nc.vector.tensor_tensor(mod[:, :, GATE, :], mod[:, :, GATE, :], gout[:, :].unsqueeze(1).broadcast_to([P, B, D]), ALU.mult).then_inc(mod_done, 1)
            dve.wait_ge(whi_ready, KC + 3)
            nc.vector.tensor_tensor(w_lo[:, :, :].rearrange("p h f -> p (h f)"), w_raw[:, :, :].rearrange("p k n -> p (k n)"),
                                    w_hi[:, :, :].rearrange("p h f -> p (h f)"), ALU.subtract).then_inc(wlo_ready, 1)

            def chunk(c):
                return slice(c * BANK, (c + 1) * BANK)

            def q_scale(n, k, bank_job):
                dve.wait_ge(x_bank_free, bank_job)
                if not (isinstance(n, int) and n == 0 and k == 0):
                    dve.wait_ge(q_rn_ready, q_job(n, k) - 1)
                nc.vector.tensor_reduce(q_ss[:, :], q_sq[:, :, :, :].rearrange("p t h d -> p (t h) d"), AX.X, ALU.add).then_inc(q_ss_ready, 1)

            def q_apply(n, k):
                dve.wait_ge(q_rn_ready, q_job(n, k))
                nc.vector.tensor_tensor(qn[:, 2 * k:2 * k + 2, :, :].rearrange("p t h d -> p (t h) d"),
                                        q_raw[:, k % 2, :, :, :].rearrange("p t h d -> p (t h) d"),
                                        q_rn[:, k % 2, :].unsqueeze(2).broadcast_to([P, 4, DH]), ALU.mult).then_inc(qn_ready, 1)

            def t_lo(hi, dst, count):
                dve.wait_ge(t_hi_ready, count)
                nc.vector.tensor_tensor(dst, pX[:, :], hi, ALU.subtract).then_inc(x_bank_free, 1)

            for b in range(B):
                for k in range(4):
                    q_scale(b, k, 6 * b + k + 1)
                    dve.wait_ge(v_hi_ready, 4 * b + k + 1)
                    nc.vector.tensor_tensor(v[b][:, LO, 2 * k:2 * k + 2, :], q_raw[:, k % 2, :, 1, :],
                                            v[b][:, HI, 2 * k:2 * k + 2, :], ALU.subtract).then_inc(v_lo_ready, 1)
                    q_apply(b, k)
                for c in range(CH):
                    t_lo(kT[b][:, HI, chunk(c)], kT[b][:, LO, chunk(c)], 2 * b + c + 1)
            for k in range(4):
                q_scale(2, k, 6 * B + k + 1)
                q_apply(2, k)
            for c in range(CH):
                t_lo(qT[:, 0, HI, chunk(c)], qT[:, 0, LO, chunk(c)], t_job(0, c))

            def o_lo(head):
                dve.wait_ge(o_hi_ready, head + 1)
                nc.vector.tensor_tensor(oT[:, LO, :].rearrange("p (c n) -> p c n", c=CH), pO[:, :, :],
                                        oT[:, HI, :].rearrange("p (c n) -> p c n", c=CH), ALU.subtract).then_inc(o_lo_ready, 1)

            def row_sums(head, parity):
                dve.wait_ge(y_job_ready, y_job(head, 0))
                nc.vector.reciprocal(rz[:, parity, :], pY[:, 0:NT]).then_inc(y_bank_free, 1)

            def add_head(head, k, parity, b, new):
                dve.wait_ge(y_job_ready, y_job(head, k + 1))
                dve.wait_ge(y_bank_free, y_job(head, 0))
                for i in range(2):
                    t = 2 * k + i
                    dst = resid[:, NT * b + t, :]
                    src = pY[:, i * D:(i + 1) * D]
                    if new:
                        ins = nc.vector.tensor_scalar(dst, src, rz[:, parity, t:t + 1], None, ALU.mult)
                    else:
                        ins = nc.vector.scalar_tensor_tensor(out=dst, in0=src, scalar=rz[:, parity, t:t + 1], in1=dst,
                                                             op0=ALU.mult, op1=ALU.add)
                ins.then_inc(y_bank_free, 1)

            def steps(it, b, first, last):
                start, end = b == 0 and first, b == B - 1 and last
                before_b = b - 1 if first else b
                for s in range(STEPS):
                    t, head, j = step(it, s), 2 * it + s // NT, s % NT
                    dve.wait_ge(p32_ready, t + 1)
                    if not (start and s < 2):
                        dve.wait_ge(pv_done, t - 1)
                    nc.vector.tensor_tensor(plo[:, s % 2, :], p32[:, s % 4, :], phi[:, s % 4, :], ALU.subtract).then_inc(plo_ready, 1)
                    if j:
                        total = psums[:, (s // NT) % 2, :]
                        if j == 1 and not start:
                            dve.wait_ge(y_job_ready, y_job(head - 2, 0))
                        if j > 1:
                            dve.wait_ge(psum_added, 7 * head + j - 1)
                        nc.vector.tensor_tensor(total, p32[:, (s - 1) % 4, :] if j == 1 else total, p32[:, s % 4, :], ALU.add).then_inc(psum_added, 1)
                    if s in B_AT:
                        c = B_AT.index(s)
                        t_lo(qT[:, 1, HI, chunk(c)], qT[:, 1, LO, chunk(c)], t_job(it, 2 + c))
                    if not end:
                        if s in Q_AT:
                            q_scale(it + 3, Q_AT.index(s), x_job(it, 2 + Q_AT.index(s)))
                        if s - 1 in Q_AT:
                            q_apply(it + 3, Q_AT.index(s - 1))
                        if s in A_AT:
                            c = A_AT.index(s)
                            t_lo(qT[:, 0, HI, chunk(c)], qT[:, 0, LO, chunk(c)], t_job(it + 1, c))
                    if not start:
                        if s == Z_B:
                            row_sums(2 * it - 1, 1)
                        if s in OB_AT:
                            add_head(2 * it - 1, OB_AT.index(s), 1, before_b, False)
                    if s == Z_A:
                        row_sums(2 * it, 0)
                    if s in OA_AT:
                        add_head(2 * it, OA_AT.index(s), 0, b, first)
                    if s == 0 and not start:
                        o_lo(2 * it - 1)
                    if s == NT:
                        o_lo(2 * it)

            dve.wait_ge(dma_scratch, 16 * 8)
            iterations(dve, steps)
            o_lo(2 * ITERS - 1)
            row_sums(2 * ITERS - 1, 1)
            for k in range(4):
                add_head(2 * ITERS - 1, k, 1, B - 1, False)

            dve.wait_ge(misc_ready, 2)
            nc.vector.tensor_tensor(router_sb[:, LO, :, :], router_raw[:, :, :], router_sb[:, HI, :, :], ALU.subtract).then_inc(misc_ready, 1)
            for i in range(3):
                dve.wait_ge(ehi_ready, i + 1)
                raw = e_raw[:, :, :] if i < 2 else down_raw
                hi, lo = [gu_w[:, i, s, :, :] if i < 2 else down_w[:, s, :, :] for s in (HI, LO)]
                nc.vector.tensor_tensor(lo, raw, hi, ALU.subtract).then_inc(elo_ready, 1)
            dve.wait_ge(y_bank_free, y_job(2 * ITERS - 1, 4))
            chain = [0]

            def link(ins):
                chain[0] += 1
                ins.then_inc(route_chain, 1)
                dve.wait_ge(route_chain, chain[0])

            for g in range(GROUPS):
                b, m = g // 2, 2 * GROUPS + 4 * g
                here = resid[:, GT * g:GT * g + GT, :]
                ln(ln_third(g), here)
                dve.wait_ge(normed, 2 * GT * GROUPS + 2 * GT * g + GT)
                nc.vector.tensor_tensor(z[:, :, :], z[:, :, :], rows(b, GATE), ALU.mult).then_inc(modulated, 1)
                dve.wait_ge(modulated, m + 1)
                dve.wait_ge(x_again_in, 16 * (g + 1))
                nc.vector.tensor_tensor(here, z[:, :, :], x_again[:, :, :], ALU.add).then_inc(modulated, 1)
                dve.wait_ge(modulated, m + 2)
                ln(ln_third(g) + 1, here)
                modulate(b, 3, m + 3, 2 * GT * GROUPS + 2 * GT * g + 2 * GT)
                transposed_lo(GROUPS + g, b, g % 2)
                dve.wait_ge(logits_ready, g + 1)
                link(nc.vector.tensor_copy(logits[:, :, :], pY[:, 0:GT * E].rearrange("p (t e) -> p t e", e=E)))
                for t in range(GT):
                    ins = nc.vector.max(top[:, t, :], logits[:, t, :])
                link(ins)
                for t in range(GT):
                    ins = nc.vector.max_index(top_at[:, t, :], top[:, t, :], logits[:, t, :])
                link(ins)
                link(nc.vector.tensor_copy(top_f[:, :, :], top_at[:, :, 0:TOPK]))
                nc.vector.tensor_tensor(r_d[:, :], top[:, :, 1], top[:, :, 0], ALU.subtract).then_inc(top_ready, 1)
                dve.wait_ge(exp_ready, g + 1)
                link(nc.vector.tensor_scalar(r_den[:, :], r_e[:, :], 1.0, None, ALU.add))
                link(nc.vector.reciprocal(r_w[:, :, 0], r_den[:, :]))
                link(nc.vector.tensor_tensor(r_w[:, :, 1], r_w[:, :, 0], r_e[:, :], ALU.mult))
                for t in range(GT):
                    nc.vector.tensor_scalar(r_one[:, t, :], experts, top_f[:, t, 0:1], r_w[:, t, 0:1], ALU.is_equal, ALU.mult)
                    ins = nc.vector.tensor_scalar(r_two[:, t, :], experts, top_f[:, t, 1:2], r_w[:, t, 1:2], ALU.is_equal, ALU.mult)
                link(ins)
                if g:
                    dve.wait_ge(rT_psum, g)
                nc.vector.tensor_tensor(route[:, :, 0:E], r_one[:, :, :], r_two[:, :, :], ALU.add)
                nc.vector.tensor_tensor(route[:, :, E:2 * E], r_one[:, :, :], r_two[:, :, :], ALU.add).then_inc(route_ready, 1)
                dve.wait_ge(rT_hi_ready, g + 1)
                nc.vector.scalar_tensor_tensor(out=rT[:, g * BANK:(g + 1) * BANK], in0=rT_hi[:, :], scalar=small[0:2 * E, P:P + 1],
                                               in1=pX[0:2 * E, :], op0=ALU.mult, op1=ALU.add).then_inc(rT_ready, 1)

            for g in range(GROUPS):
                for t in range(RT):
                    n = RT * g + t
                    dve.wait_ge(silu_done, n + 1)
                    if n:
                        dve.wait_ge(a_done, n)
                    nc.vector.tensor_tensor(act_u[:, :], act_s[:, t % 2, :], pS[:, t % 2, 1, :], ALU.mult).then_inc(u_done, 1)
                    dve.wait_ge(u_done, n + 1)
                    dve.wait_ge(cw_ready, n + 1)
                    if before(g, t) > 0:
                        dve.wait_ge(ahi_done, before(g, t))
                    nc.vector.tensor_tensor(act_a[:, t % 2, :], act_u[:, :], pX[:, :], ALU.mult).then_inc(a_done, 1)
                    dve.wait_ge(ahi_done, n + 1)
                    nc.vector.tensor_tensor(act_lo[:, t % 2, :], act_a[:, t % 2, :], act_hi[:, t % 2, :], ALU.subtract).then_inc(alo_done, 1)
                dve.wait_ge(down_done, RT * (g + 1))
                if g:
                    dve.wait_ge(dma_out, 16 * g)
                nc.vector.tensor_tensor(o_sb[:, :, :], pO[:, :, :].rearrange("p c (t f) -> p (c t) f", f=D), rows(g // 2, 3 + GATE), ALU.mult).then_inc(o_mul, 1)
                dve.wait_ge(o_mul, g + 1)
                nc.vector.tensor_tensor(o_sb[:, :, :], o_sb[:, :, :], resid[:, GT * g:GT * g + GT, :], ALU.add).then_inc(o_done, 1)

        @block.tensor
        def _(pe):
            pe.wait_ge(silu_ready, 1)
            pe.wait_ge(dma_wmod, 16)
            for c in range(3):
                for b in range(B):
                    i = B * c + b
                    dst = pS[:, i // 2, i % 2, :] if i < 4 else pO[:, i % 2, :]
                    for k in range(KC):
                        mm = pe.matmul(dst, silu_rows[:, k, b, :], wmod_sb[:, k, c * BANK:(c + 1) * BANK], start=(k == 0), stop=(k == KC - 1))
                    mm.then_inc(mod_ready, 1)
            pe.wait_ge(dma_const, 16 * 3)

            def transpose_group(i):
                for k in range(KC):
                    if i:
                        pe.wait_ge(xt_lo_ready, KC * (i - 1) + k + 1)
                    for t in range(GT):
                        mm = pe.transpose(pS[:, 0, k, t * P:(t + 1) * P], z[:, t, k * P:(k + 1) * P], ident)
                    mm.then_inc(xt_ready, 1)

            pe.wait_ge(mod_copied, 6)
            for g in range(GROUPS):
                pe.wait_ge(normed, 2 * GT * (g + 1))
                transpose_group(g)

            def project(n, k, b, w, job, free):
                if free:
                    pe.wait_ge(x_bank_free, job - 1)
                for i in range(2):
                    t = 2 * k + i
                    for p, (s, m) in enumerate(PASSES):
                        for c in range(KC):
                            mm = pe.matmul(pX[:, i * D:(i + 1) * D], xT[b][:, s, c, t * P:(t + 1) * P], w[:, m, c, :],
                                           start=(p == 0 and c == 0), stop=(p == 2 and c == KC - 1))
                mm.then_inc(x_job_ready, 1)

            def transpose_head(h, c, job):
                pe.wait_ge(x_bank_free, job - 1)
                for i in range(GT):
                    mm = pe.transpose(pX[:, i * P:(i + 1) * P], qn[:, GT * c + i, h, :], ident)
                mm.then_inc(x_job_ready, 1)

            pe.wait_ge(wlo_ready, KC)
            for b in range(B):
                pe.wait_ge(xt_lo_ready, 2 * KC * (b + 1))
                for k in range(4):
                    project(b, k, b, wkv_sb, 6 * b + k + 1, b or k)
                pe.wait_ge(qn_ready, q_job(b, 3))
                for c in range(CH):
                    transpose_head(0, c, 6 * b + 4 + c + 1)
            pe.wait_ge(wq_in, 16)
            for k in range(4):
                project(2, k, 0, wq_sb, 6 * B + k + 1, True)
            pe.wait_ge(qn_ready, q_job(2, 3))
            for c in range(CH):
                transpose_head(0, c, 6 * B + 4 + c + 1)

            def scores(b, s):
                h, j = (s // NT) % 2, s % NT
                for p, (a, m) in enumerate(PASSES):
                    for c in range(CH):
                        mm = pe.matmul(pS[:, s % 2, c, :], kT[b][:, a, j * P:(j + 1) * P], qT[:, h, m, c * BANK:(c + 1) * BANK],
                                       start=(p == 0), stop=(p == 2))
                mm.then_inc(scores_ready, 1)

            def weighted_values(it, b, s, fresh):
                j = s % NT
                pe.wait_ge(phi_ready, step(it, s) + 1)
                if j == 0 and not fresh:
                    pe.wait_ge(o_lo_ready, 2 * it + s // NT)
                for p, (a, m) in enumerate(((LO, HI), (HI, HI), (HI, LO))):
                    if m == LO:
                        pe.wait_ge(plo_ready, step(it, s) + 1)
                    moving = phi[:, s % 4, :] if m == HI else plo[:, s % 2, :]
                    for c in range(CH):
                        mm = pe.matmul(pO[:, c, :], v[b][:, a, j, :], moving[:, c * BANK:(c + 1) * BANK],
                                       start=(j == 0 and p == 0), stop=(j == NT - 1 and p == 2))
                mm.then_inc(pv_done, 1)

            def sums(head, parity, free):
                pe.wait_ge(psum_added, 7 * (head + 1))
                if free:
                    pe.wait_ge(y_bank_free, y_job(head - 1, 4))
                for t in range(NT):
                    mm = pe.matmul(pY[:, t:t + 1], psums[:, parity, t * P:(t + 1) * P], ones[:, :], start=True, stop=True)
                mm.then_inc(y_job_ready, 1)

            def project_out(head, k, parity, landed, count):
                pe.wait_ge(y_bank_free, y_job(head, k))
                if k == 0:
                    pe.wait_ge(o_lo_ready, head + 1)
                    pe.wait_ge(landed, count)
                for i in range(2):
                    t = 2 * k + i
                    for p, (a, m) in enumerate(PASSES):
                        mm = pe.matmul(pY[:, i * D:(i + 1) * D], oT[:, a, t * P:(t + 1) * P], wout_sb[parity][:, m, :], start=(p == 0), stop=(p == 2))
                mm.then_inc(y_job_ready, 1)

            pe.wait_ge(x_bank_free, 6 * B + 6)
            scores(0, 0)

            def steps(it, b, first, last):
                start, end = b == 0 and first, b == B - 1 and last
                q_batch = b + 1 if last else b
                for s in range(STEPS):
                    if not (end and s == STEPS - 1):
                        if not (start and s == 0):
                            pe.wait_ge(p32_ready, step(it, s))
                        if s == NT - 1:
                            pe.wait_ge(x_bank_free, x_job(it, 1))
                        if s == STEPS - 1:
                            pe.wait_ge(x_bank_free, x_job(it, 7))
                        scores(q_batch if s == STEPS - 1 else b, s + 1)
                    if s in B_AT:
                        transpose_head(1, B_AT.index(s), x_job(it, B_AT.index(s)))
                    if not end:
                        if s in Q_AT:
                            k = Q_AT.index(s)
                            if k == 0:
                                pe.wait_ge(wq_in, 16 * (it + 2))
                            project(it + 3, k, q_batch, wq_sb, x_job(it, 2 + k), True)
                        if s in A_AT:
                            if s == A_AT[0]:
                                pe.wait_ge(qn_ready, q_job(it + 3, 3))
                            transpose_head(0, A_AT.index(s), x_job(it, 6 + A_AT.index(s)))
                    if not start:
                        if s == Z_B:
                            sums(2 * it - 1, 1, True)
                        if s in OB_AT:
                            project_out(2 * it - 1, OB_AT.index(s), 1, woutb_in, 16 * it)
                    if s == Z_A:
                        sums(2 * it, 0, not start)
                    if s in OA_AT:
                        project_out(2 * it, OA_AT.index(s), 0, wouta_in, 16 * (it + 1))
                    if s:
                        weighted_values(it, b, s - 1, start and s == 1)
                    elif not start:
                        weighted_values(it - 1, b - 1 if first else b, STEPS - 1, False)

            iterations(pe, steps)
            weighted_values(ITERS - 1, B - 1, STEPS - 1, False)
            sums(2 * ITERS - 1, 1, True)
            for k in range(4):
                project_out(2 * ITERS - 1, k, 1, woutb_in, 16 * ITERS)

            pe.wait_ge(misc_ready, 3)
            for g in range(GROUPS):
                pe.wait_ge(modulated, 2 * GROUPS + 4 * g + 4)
                if g == 0:
                    pe.wait_ge(p32_ready, STEPS * ITERS)
                transpose_group(GROUPS + g)
                pe.wait_ge(xt_lo_ready, KC * (GROUPS + g + 1))
                pe.wait_ge(y_bank_free, y_job(2 * ITERS - 1, 4))
                if g:
                    pe.wait_ge(top_ready, g)
                for t in range(GT):
                    at = (g % 2) * BANK + t * P
                    for p, (a, m) in enumerate(PASSES):
                        for c in range(KC):
                            mm = pe.matmul(pY[:, t * E:(t + 1) * E], xT[g // 2][:, a, c, at:at + P], router_sb[:, m, c, :],
                                           start=(p == 0 and c == 0), stop=(p == 2 and c == KC - 1))
                mm.then_inc(logits_ready, 1)
                pe.wait_ge(route_ready, g + 1)
                if g:
                    pe.wait_ge(rT_ready, g)
                for t in range(GT):
                    mm = pe.transpose(pX[0:2 * E, t * P:(t + 1) * P], route[:, t, :], ident)
                mm.then_inc(rT_psum, 1)

            pe.wait_ge(elo_ready, 3)
            pe.wait_ge(rT_ready, GROUPS)

            def up(g, t):
                n = RT * g + t
                if before(g, t) > 0:
                    pe.wait_ge(u_done, before(g, t))
                for u in range(2):
                    for p, (a, m) in enumerate(PASSES):
                        for c in range(KC):
                            mm = pe.matmul(pS[:, t % 2, u, :], gu_w[:, u, a, c, t * P:(t + 1) * P],
                                           xT[g // 2][:, m, c, (g % 2) * BANK:(g % 2 + 1) * BANK],
                                           start=(p == 0 and c == 0), stop=(p == 2 and c == KC - 1))
                mm.then_inc(gu_ready, 1)
                if n:
                    pe.wait_ge(a_done, n)
                pe.matmul(pX[:, :], select[:, t * P:(t + 1) * P], rT[:, g * BANK:(g + 1) * BANK], start=True, stop=True).then_inc(cw_ready, 1)

            def down(g, t):
                pe.wait_ge(alo_done, RT * g + t + 1)
                if t == 0 and g:
                    pe.wait_ge(o_mul, g)
                for i in range(GT):
                    for p, (a, m) in enumerate(PASSES):
                        w = (act_hi, act_lo)[a][:, t % 2, i * P:(i + 1) * P]
                        mm = pe.matmul(pO[:, i // 2, (i % 2) * D:(i % 2 + 1) * D], w, down_w[:, m, t, :],
                                       start=(t == 0 and p == 0 and i % 2 == 0), stop=(t == RT - 1 and p == 2), skip_group_check=True)
                mm.then_inc(down_done, 1)

            up(0, 0)
            for g in range(GROUPS):
                for t in range(RT):
                    if t + 1 < RT:
                        up(g, t + 1)
                    elif g + 1 < GROUPS:
                        up(g + 1, 0)
                    down(g, t)


B_AT = [0, 2]
Q_AT = [3, 5, 7, 9]
A_AT = [12, 13]
Z_B, Z_A = 1, 10
OB_AT = [2, 3, 4, 6]
OA_AT = [11, 12, 13, 14]


def before(g, t):
    return RT * g + t - 1 if t >= 2 else RT * g - t


def kernel(**inputs):
    import concourse.bacc as bacc
    from concourse.bass_utils import run_bass_kernel_spmd

    w1 = np.asarray(inputs["L0_ffn_w1"])
    laid_out = {
        "x": np.asarray(inputs["L0_attn_x"]),
        "g_norm": np.asarray(inputs["L0_attn_g_norm"]).reshape(KC, P).T,
        "wq": np.asarray(inputs["L0_attn_Wq"]),
        "wkv": np.asarray(inputs["L0_attn_Wkv"]),
        "wout": np.asarray(inputs["L0_attn_Wout"]),
        "g_out": np.asarray(inputs["L0_attn_g_out"]),
        "router": np.asarray(inputs["L0_ffn_router_w"]).T,
        "w_gate": w1[:, :INNER].reshape(ROWS, D).T,
        "w_up": w1[:, INNER:].reshape(ROWS, D).T,
        "w_down": np.asarray(inputs["L0_ffn_w2"]).transpose(0, 2, 1).reshape(ROWS, D),
        "cond": np.asarray(inputs["L0_c"]).T.reshape(KC, P, B).transpose(1, 0, 2),
        "wmod": np.asarray(inputs["L0_wmod"]),
        "consts": shape_constants(),
    }
    nc = bacc.Bacc("TRN2", target_bir_lowering=False, num_devices=1)
    arrays, args = {}, []
    for name, a in laid_out.items():
        a = np.ascontiguousarray(a)
        arrays[f"in_{name}"] = a
        args.append(nc.dram_tensor(f"in_{name}", a.shape, mybir.dt.from_np(a.dtype), kind="ExternalInput").ap())
    args.append(nc.dram_tensor("out_x", (B, N, D), F32, kind="ExternalOutput").ap())
    adaln_block(nc, *args)
    return run_bass_kernel_spmd(nc, [arrays], core_ids=[0]).results[0]["out_x"]
```

```python
from contextlib import ExitStack

import numpy as np

import concourse.bass as bass
from concourse import mybir

P = 128
BANK = 512
B, N, D = 2, 1024, 256
EPS_LN = 1e-5
EPS_Q = 1e-12 / 256.0
EPS_K = 1e-12
POOL_CONSTANTS = (-0.5, 1.5, EPS_LN, EPS_K, EPS_Q)
KC = D // P
HEADS, DH = 16, 128
PAIRS = HEADS // 2
NT = N // P
CH = N // BANK
STEPS = 2 * NT
ITERS = B * PAIRS
E, TOPK, INNER = 8, 2, 176
ROWS = E * INNER
RT = ROWS // P
GROUPS = B * N // BANK
GT = BANK // P
TILE = 2 * KC * P + D
SMALL = P + 1 + E
SHIFT, SCALE, GATE = 0, 1, 2

F32 = mybir.dt.float32
F32R = mybir.dt.float32r
U32 = mybir.dt.uint32
ALU = mybir.AluOpType
ACT = mybir.ActivationFunctionType
AX = mybir.AxisListType

HI, LO = 0, 1
PASSES = ((LO, HI), (HI, HI), (HI, LO))


def shape_constants():
    select = np.zeros((P, ROWS), np.float32)
    for k in range(2 * E):
        select[k, (k % E) * INNER:(k % E + 1) * INNER] = 1.0
    not_hi = np.zeros((P, 1), np.float32)
    not_hi[E:2 * E] = -1.0
    experts = np.tile(np.arange(E, dtype=np.float32), (P, 1))
    return np.concatenate([np.eye(P, dtype=np.float32), not_hi, experts, select], axis=1)


def adaln_block(nc, x, g_norm, wq, wkv, wout, g_out, router, experts_w, cond, wmod,
                consts, out):
    ctx = ExitStack()
    with ctx:
        def sb(name, shape, dt=F32, where=ctx):
            return where.enter_context(nc.sbuf_tensor(name, shape, dt))

        def sem(name):
            return ctx.enter_context(nc.semaphore(name))

        small = sb("small", [P, SMALL])
        ident = small[:, 0:P]
        experts = small[:, P + 1:SMALL]
        ones = sb("ones", [P, 1])
        mod = sb("mod", [P, B, 6, D])
        gout = sb("gout", [P, D])
        gate_sign = sb("gate_sign", [P, B, D])
        gnorm = sb("gnorm", [P, KC])
        condT = sb("condT", [P, KC, B])
        cond_e = sb("cond_e", [P, KC, B])
        silu_rows = sb("silu_rows", [P, KC, B, P])
        resid = sb("resid", [P, B * NT, D])
        xT = [sb(f"xT{b}", [P, 2, KC, N], F32R) for b in range(B)]
        LNS = 4 * GROUPS
        ln_stats = sb("ln_stats", [P, LNS, GT, 6])
        ln_mv = sb("ln_mv", [P, LNS, GT, 2])
        ln_r = sb("ln_r", [P, LNS, GT])
        ln_nb = sb("ln_nb", [P, LNS, GT])
        ln_t = sb("ln_t", [P, 3, GT])
        pool_c = sb("pool_c", [P, len(POOL_CONSTANTS), GT])
        z = sb("z", [P, GT, D])
        q_ss = sb("q_ss", [P, 4])
        q_t = sb("q_t", [P, 3, 4])
        q_rn = sb("q_rn", [P, 2, 4])
        rz = sb("rz", [P, 2, NT])
        router_raw = sb("router_raw", [P, KC, E])
        router_sb = sb("router_sb", [P, 2, KC, E], F32R)
        logits = sb("logits", [P, GT, E])
        top = sb("top", [P, GT, 8])
        top_at = sb("top_at", [P, GT, 8], U32)
        top_f = sb("top_f", [P, GT, TOPK])
        r_d = sb("r_d", [P, GT])
        r_e = sb("r_e", [P, GT])
        r_den = sb("r_den", [P, GT])
        r_w = sb("r_w", [P, GT, TOPK])
        r_one = sb("r_one", [P, GT, E])
        r_two = sb("r_two", [P, GT, E])
        route = sb("route", [P, GT, 2 * E])

        early = ExitStack()
        wmod_sb = sb("wmod_sb", [P, KC, 6 * D], where=early)
        w_raw = sb("w_raw", [P, KC, HEADS * DH], where=early)
        w_hi = sb("w_hi", [P, 2 * PAIRS, KC * D // 2], F32R, where=early)
        w_lo = sb("w_lo", [P, 2 * PAIRS, KC * D // 2], F32R, where=early)
        early.close()

        mid = ExitStack()
        psums = sb("psums", [P, 2, N], where=mid)
        oT = sb("oT", [P, 2, N], F32R, where=mid)
        wout_sb = [sb(f"wout_sb{h}", [P, 2, D], F32R, where=mid) for h in range(2)]
        p32 = sb("p32", [P, 4, N], where=mid)
        phi = sb("phi", [P, 4, N], F32R, where=mid)
        plo = sb("plo", [P, 2, N], F32R, where=mid)
        kT1 = sb("kT1", [P, 2, N], F32R, where=mid)
        v1 = sb("v1", [P, 2, NT, DH], F32R, where=mid)
        qT = sb("qT", [P, 2, 2, N], F32R, where=mid)
        qn = sb("qn", [P, NT, 2, DH], where=mid)
        q_raw = sb("q_raw", [P, 2, 2, 2, DH], where=mid)
        q_sq = sb("q_sq", [P, 2, 2, DH], where=mid)
        wq_sb = sb("wq_sb", [P, 2, KC, D], F32R, where=mid)
        kT0 = sb("kT0", [P, 2, N], F32R, where=mid)
        v0 = sb("v0", [P, 2, NT, DH], F32R, where=mid)
        wkv_sb = sb("wkv_sb", [P, 2, KC, D], F32R, where=mid)
        wkv_raw = sb("wkv_raw", [P, KC, 2 * DH], where=mid)
        mid.close()
        kT, v = [kT0, kT1], [v0, v1]

        late = ExitStack()
        sb("still_used", [P, 2 * N + 2 * N + 2 * 2 * D], where=late)
        expert_w = sb("expert_w", [P, RT, 2, TILE], F32R, where=late)
        act_s = sb("act_s", [P, 2, BANK], where=late)
        act_u = sb("act_u", [P, BANK], where=late)
        act_a = sb("act_a", [P, 2, BANK], where=late)
        act_hi = sb("act_hi", [P, 2, BANK], F32R, where=late)
        act_lo = sb("act_lo", [P, 2, BANK], F32R, where=late)
        o_sb = sb("o_sb", [P, GT, D], where=late)
        loop_only = 10 * N + 2 * N + 2 * NT * DH + 4 * N + NT * 2 * DH + 8 * DH + 4 * DH + 2 * KC * D
        sb("up_to_kT0", [P, loop_only - RT * 2 * TILE - 9 * BANK - GT * D], where=late)
        x_again = sb("x_again", [P, GT, D], where=late)
        rT = sb("rT", [2 * E, 2, BANK], F32R, where=late)
        rT_hi = sb("rT_hi", [2 * E, BANK], F32R, where=late)
        select = sb("select", [2 * E, ROWS], F32R, where=late)
        logits_T = sb("logits_T", [E, BANK], where=late)
        e_raw = sb("e_raw", [P, 2, TILE], where=late)
        late.close()

        pS = ctx.enter_context(nc.psum_tensor("pS", [P, 2, CH, BANK], F32))
        pO = ctx.enter_context(nc.psum_tensor("pO", [P, CH, BANK], F32))
        pX = ctx.enter_context(nc.psum_tensor("pX", [P, BANK], F32))
        pY = ctx.enter_context(nc.psum_tensor("pY", [P, BANK], F32))

        wq_split = nc.dram_tensor("wq_split", [ITERS, P, 2, KC * D], F32, kind="Internal").ap()
        wout_split = nc.dram_tensor("wout_split", [2 * ITERS, P, 2, D], F32, kind="Internal").ap()
        select_dram = nc.dram_tensor("select_dram", [2 * E, ROWS], F32, kind="Internal").ap()

        (dma_c, dma_const, dma_wmod, dma_wq, dma_wkv, dma_wout, dma_scratch, dma_out,
         wq_in, wouta_in, woutb_in, dma_router, dma_select, select_in) = map(sem, (
             "dma_c dma_const dma_wmod dma_wq dma_wkv dma_wout dma_scratch dma_out "
             "wq_in wouta_in woutb_in dma_router dma_select select_in").split())
        e_raw_in = [sem(f"e_raw_in{i}") for i in range(2)]
        dma_x = [sem(f"dma_x{g}") for g in range(GROUPS)]
        x_again_in = sem("x_again_in")
        (cond_exp, cond_den, silu_ready, mod_ready, mod_copied, mod_done) = map(sem, (
            "cond_exp cond_den silu_ready mod_ready mod_copied mod_done").split())
        constants_made = sem("constants_made")
        (ln_sem, stats_ready, rstd_chain, rstd_ready, normed, modulated) = map(sem, (
            "ln_sem stats_ready rstd_chain rstd_ready normed modulated").split())
        (whi_ready, wlo_ready) = map(sem, "whi_ready wlo_ready".split())
        (x_job_ready, x_bank_free) = map(sem, "x_job_ready x_bank_free".split())
        (q_copied, q_ss_ready, q_chain, q_rn_ready, qn_ready, t_hi_ready, t_lo_ready) = map(sem, (
            "q_copied q_ss_ready q_chain q_rn_ready qn_ready t_hi_ready t_lo_ready").split())
        (v_hi_ready, v_lo_ready) = map(sem, "v_hi_ready v_lo_ready".split())
        (scores_ready, phi_ready, p32_ready, plo_ready, psum_added, pv_done) = map(sem, (
            "scores_ready phi_ready p32_ready plo_ready psum_added pv_done").split())
        (o_hi_ready, o_lo_ready, y_job_ready, y_bank_free) = map(sem, (
            "o_hi_ready o_lo_ready y_job_ready y_bank_free").split())
        (xt_ready, xt_hi_ready, xt_lo_ready) = map(sem, "xt_ready xt_hi_ready xt_lo_ready".split())
        (top_ready, route_chain, exp_ready, route_ready, rT_hi_ready) = map(sem, (
            "top_ready route_chain exp_ready route_ready rT_hi_ready").split())
        (router_hi, router_lo, gu_ready, cw_ready, silu_done, u_done, a_done, ahi_done, alo_done, down_done, o_mul,
         o_done, ehi_ready, elo_ready) = map(sem, (
             "router_hi router_lo gu_ready cw_ready silu_done u_done a_done ahi_done alo_done down_done o_mul "
             "o_done ehi_ready elo_ready").split())

        def q_job(n, k):
            return 4 * n + k + 1

        def t_job(n, k):
            return 2 * B + 4 * n + k + 1

        def x_job(it, k):
            return 6 * B + 6 + 8 * it + k + 1

        def between_job(g, k):
            return x_job(ITERS - 1, 2 + 5 * g + k)

        def y_job(head, k):
            return 5 * head + k + 1

        def added(it, s):
            it, s = it + s // STEPS, s % STEPS
            return 7 * (2 * it + s // NT) + max(s % NT, 1)

        def step(it, s):
            return STEPS * it + s

        def ln_first(g):
            return 2 * g

        def ln_third(g):
            return 2 * GROUPS + 2 * g

        tokens = x.rearrange("b (t p) f -> p (b t) f", p=P)
        out_tokens = out.rearrange("b (t p) f -> p (b t) f", p=P)

        def iterations(eng, body):
            for b in range(B):
                body(PAIRS * b, b, True, False)
                with eng.Fori(PAIRS * b + 1, PAIRS * b + PAIRS - 1) as it:
                    body(it, b, False, False)
                body(PAIRS * b + PAIRS - 1, b, False, True)

        block = ctx.enter_context(nc.Block())

        @block.sync
        def _(sp):
            sp.dma_start(condT[:, :, :], cond).then_inc(dma_c, 16)
            for g in range(GROUPS):
                sp.dma_start(resid[:, GT * g:GT * g + GT, :], tokens[:, GT * g:GT * g + GT, :]).then_inc(dma_x[g], 16)
                if g == 0:
                    sp.dma_start(wmod_sb[:, :, :], wmod.rearrange("(k p) n -> p k n", p=P)).then_inc(dma_wmod, 16)
            sp.dma_start(router_raw[:, :, :], router.rearrange("(k p) e -> p k e", p=P)).then_inc(dma_router, 16)
            sp.dma_start(select_dram, consts[0:2 * E, SMALL:SMALL + ROWS]).then_inc(dma_select, 16)
            sp.dma_start(small[:, :], consts[:, 0:SMALL]).then_inc(dma_const, 16)
            sp.dma_start(gnorm[:, :], g_norm).then_inc(dma_const, 16)
            sp.dma_start(gout[:, :], g_out.rearrange("(a f) -> a f", a=1).broadcast_to([P, D])).then_inc(dma_const, 16)

            sp.dma_start(wkv_raw[:, :, :], wkv.rearrange("(k p) n -> p k n", p=P)).then_inc(dma_wkv, 16)
            sp.dma_start(w_raw[:, :, :], wq.rearrange("(k p) n -> p k n", p=P)).then_inc(dma_wq, 16)
            sp.wait_ge(whi_ready, KC + 2)
            sp.wait_ge(wlo_ready, KC + 2)
            for b in range(B):
                for part, w in ((HI, w_hi), (LO, w_lo)):
                    dst = wq_split[PAIRS * b:PAIRS * b + PAIRS, :, part, :].rearrange("n p f -> p n f")
                    sp.dma_start(dst, w[:, :, :].rearrange("p (n a) f -> p n (a f)", a=2).bitcast(F32)).then_inc(dma_scratch, 16)
            sp.dma_start(w_raw[:, :, :].rearrange("p k (h n) -> p (k h) n", n=D),
                         wout.rearrange("(h d) n -> d h n", d=DH)).then_inc(dma_wout, 16)
            sp.wait_ge(whi_ready, KC + 3)
            sp.wait_ge(wlo_ready, KC + 3)
            for b in range(B):
                for part, w in ((HI, w_hi), (LO, w_lo)):
                    dst = wout_split[HEADS * b:HEADS * b + HEADS, :, part, :].rearrange("n p f -> p n f")
                    sp.dma_start(dst, w[:, :, :].bitcast(F32)).then_inc(dma_scratch, 16)
            sp.wait_ge(dma_scratch, 16 * 8)

            def load_wq(n):
                sp.dma_start(wq_sb[:, :, :, :].rearrange("p s k f -> p s (k f)").bitcast(F32),
                             wq_split[n, :, :, :] if isinstance(n, int) else
                             wq_split[bass.ds(n, 1), :, :, :].rearrange("n p s f -> p (n s) f")).then_inc(wq_in, 16)

            def load_wout(head, buf, landed):
                sp.dma_start(wout_sb[buf][:, :, :].bitcast(F32),
                             wout_split[head, :, :, :] if isinstance(head, int) else
                             wout_split[bass.ds(head, 1), :, :, :].rearrange("n p s f -> p (n s) f")).then_inc(landed, 16)

            load_wq(0)
            load_wout(0, 0, wouta_in)
            sp.wait_ge(q_copied, q_job(2, 3))
            load_wq(1)

            def loads(it, b, first, last):
                if not (first and b == 0):
                    sp.wait_ge(y_bank_free, y_job(2 * it - 1, 4))
                load_wout(2 * it + 1, 1, woutb_in)
                if not (b == B - 1 and last):
                    sp.wait_ge(q_copied, q_job(2 + it + 1, 3))
                    if not isinstance(it, int) or it + 2 < ITERS:
                        load_wq(it + 2)
                    sp.wait_ge(y_bank_free, y_job(2 * it, 4))
                    load_wout(2 * it + 2, 0, wouta_in)

            def load_x_again(g):
                if g:
                    sp.wait_ge(modulated, 2 * GROUPS + 4 * g - 2)
                sp.dma_start(x_again[:, :, :], tokens[:, GT * g:GT * g + GT, :]).then_inc(x_again_in, 16)

            def load_expert(t):
                sp.dma_start(e_raw[:, t % 2, :], experts_w[t, :, :]).then_inc(e_raw_in[t % 2], 16)

            for b in range(B):
                loads(PAIRS * b, b, True, False)
                with sp.Fori(PAIRS * b + 1, PAIRS * b + PAIRS - 2) as it:
                    loads(it, b, False, False)
                loads(PAIRS * b + PAIRS - 2, b, False, False)
                if b == B - 1:
                    sp.wait_ge(y_bank_free, y_job(2 * (ITERS - 1) - 2, 4))
                    load_x_again(0)
                    sp.wait_ge(dma_select, 16)
                    sp.dma_start(select[:, :].bitcast(F32), select_dram).then_inc(select_in, 16)
                    for t in range(2):
                        load_expert(t)
                loads(PAIRS * b + PAIRS - 1, b, False, True)
            load_x_again(1)
            for t in range(2, RT):
                sp.wait_ge(elo_ready, t - 1)
                load_expert(t)
            for g in range(2, GROUPS):
                load_x_again(g)
            for g in range(GROUPS):
                sp.wait_ge(o_done, g + 1)
                sp.dma_start(out_tokens[:, GT * g:GT * g + GT, :], o_sb[:, :, :]).then_inc(dma_out, 16)
            sp.wait_ge(dma_out, 16 * GROUPS)

        @block.gpsimd
        def _(pool):
            minus_half, three_halves, eps_ln, eps_k, eps_q = (pool_c[:, i, :] for i in range(len(POOL_CONSTANTS)))
            for i, value in enumerate(POOL_CONSTANTS):
                nc.gpsimd.memset(pool_c[:, i, :], value).then_inc(constants_made, 1)
            nc.gpsimd.memset(ones[:, :], 1.0).then_inc(constants_made, 1)
            pool.wait_ge(constants_made, len(POOL_CONSTANTS) + 1)
            def newton(value, eps, t, dst, done, count):
                steps = (
                    lambda: nc.gpsimd.tensor_tensor(t[0], value, eps, ALU.add),
                    lambda: nc.gpsimd.tensor_tensor(t[1], t[0], minus_half, ALU.pow),
                    lambda: nc.gpsimd.tensor_tensor(t[2], t[1], t[1], ALU.mult),
                    lambda: nc.gpsimd.tensor_tensor(t[2], t[2], t[0], ALU.mult),
                    lambda: nc.gpsimd.tensor_tensor(t[2], t[2], minus_half, ALU.mult),
                    lambda: nc.gpsimd.tensor_tensor(t[2], t[2], three_halves, ALU.add),
                )
                for i, make in enumerate(steps):
                    make().then_inc(done, 1)
                    pool.wait_ge(done, count + i + 1)
                return nc.gpsimd.tensor_tensor(dst, t[1], t[2], ALU.mult)

            def rstd(n):
                pool.wait_ge(stats_ready, n + 1)
                t = [ln_t[:, i, :] for i in range(3)]
                newton(ln_mv[:, n, :, 1], eps_ln, t, ln_r[:, n, :], rstd_chain, 8 * n).then_inc(rstd_chain, 1)
                pool.wait_ge(rstd_chain, 8 * n + 7)
                nc.gpsimd.tensor_tensor(t[0], ln_mv[:, n, :, 0], ln_r[:, n, :], ALU.mult).then_inc(rstd_chain, 1)
                pool.wait_ge(rstd_chain, 8 * n + 8)
                nc.gpsimd.tensor_scalar(ln_nb[:, n, :], t[0], -1.0, None, ALU.mult).then_inc(rstd_ready, 1)
                pool.wait_ge(rstd_ready, n + 1)

            def q_norm(n, k, eps):
                pool.wait_ge(q_ss_ready, q_job(n, k))
                if not (isinstance(n, int) and n == 0 and k < 2):
                    pool.wait_ge(qn_ready, q_job(n, k) - 2)
                newton(q_ss[:, :], eps, [q_t[:, i, :] for i in range(3)], q_rn[:, k % 2, :],
                       q_chain, 6 * (q_job(n, k) - 1)).then_inc(q_rn_ready, 1)
                pool.wait_ge(q_rn_ready, q_job(n, k))

            for g in range(GROUPS):
                for n in (ln_first(g), ln_first(g) + 1):
                    rstd(n)
            for n in range(B + 1):
                for k in range(4):
                    q_norm(n, k, eps_k if n < B else eps_q)

            def norms(it, b, first, last):
                if not (b == B - 1 and last):
                    for k in range(4):
                        q_norm(it + 3, k, eps_q)

            iterations(pool, norms)
            for g in range(GROUPS):
                for n in (ln_third(g), ln_third(g) + 1):
                    rstd(n)

        @block.scalar
        def _(act):
            act.wait_ge(dma_c, 16)
            nc.scalar.activation(cond_e[:, :, :], condT[:, :, :], ACT.Exp, scale=-1.0).then_inc(cond_exp, 1)
            for c in range(3):
                for b in range(B):
                    i = B * c + b
                    act.wait_ge(mod_ready, i + 1)
                    src = (pS[:, i // 2, i % 2, :] if i < 4 else pO[:, i % 2, :]).rearrange("p (a f) -> p a f", a=2)
                    nc.scalar.copy(mod[:, b, 2 * c:2 * c + 2, :], src).then_inc(mod_copied, 1)
            act.wait_ge(dma_const, 16 * 3)
            act.wait_ge(dma_wkv, 16)
            for k in range(KC):
                nc.scalar.activation(wkv_sb[:, HI, k, :], wkv_raw[:, k, :], ACT.Copy, scale=gnorm[:, k:k + 1]).then_inc(whi_ready, 1)

            def normalise(n, src):
                act.wait_ge(rstd_ready, n + 1)
                for t in range(GT):
                    nc.scalar.activation(z[:, t, :], src[:, t, :], ACT.Identity, scale=ln_r[:, n, t:t + 1],
                                         bias=ln_nb[:, n, t:t + 1]).then_inc(normed, 1)

            def transposed_hi(i, b, c):
                for k in range(KC):
                    act.wait_ge(xt_ready, KC * i + k + 1)
                    nc.scalar.copy(xT[b][:, HI, k, c * BANK:(c + 1) * BANK], pS[:, 0, k, :]).then_inc(xt_hi_ready, 1)

            act.wait_ge(dma_router, 16)
            nc.scalar.copy(router_sb[:, HI, :, :], router_raw[:, :, :]).then_inc(router_hi, 1)
            for g in range(GROUPS):
                if g:
                    act.wait_ge(xt_ready, KC * g)
                normalise(ln_first(g), resid[:, GT * g:GT * g + GT, :])
                normalise(ln_first(g) + 1, z)
                transposed_hi(g, g // 2, g % 2)
                if g == 0:
                    act.wait_ge(dma_wq, 16)
                    for k in range(KC):
                        nc.scalar.activation(
                            w_hi[:, :, :].rearrange("p (n a) f -> p a n f", a=2)[:, k], w_raw[:, k, :].rearrange("p (n f) -> p n f", f=D),
                            ACT.Copy, scale=gnorm[:, k:k + 1]).then_inc(whi_ready, 1)
            act.wait_ge(dma_wout, 16)
            act.wait_ge(dma_scratch, 16 * 4)
            nc.scalar.copy(w_hi[:, :, :].rearrange("p h f -> p (h f)"), w_raw[:, :, :].rearrange("p k n -> p (k n)")).then_inc(whi_ready, 1)

            def q_copy(n, k, bank_job):
                act.wait_ge(x_job_ready, bank_job)
                if not (isinstance(n, int) and n == 0 and k < 2):
                    act.wait_ge(qn_ready, q_job(n, k) - 2)
                if isinstance(n, int) and n < B and not (n == 0 and k < 2):
                    act.wait_ge(v_lo_ready, 4 * n + k - 1)
                if isinstance(n, int) and n == B and k < 2:
                    act.wait_ge(v_lo_ready, 4 * n + k - 1)
                src = pX[:, :].rearrange("p (t h d) -> p t h d", t=2, h=2)
                nc.scalar.copy(q_raw[:, k % 2, :, :, :], src).then_inc(q_copied, 1)
                if not (isinstance(n, int) and n == 0 and k == 0):
                    act.wait_ge(q_ss_ready, q_job(n, k) - 1)
                nc.scalar.activation(q_sq[:, :, :, :], src, ACT.Square).then_inc(x_bank_free, 1)

            def t_hi(dst, bank_job):
                act.wait_ge(x_job_ready, bank_job)
                nc.scalar.copy(dst, pX[:, :]).then_inc(t_hi_ready, 1)

            def chunk(c):
                return slice(c * BANK, (c + 1) * BANK)

            for b in range(B):
                for k in range(4):
                    q_copy(b, k, 6 * b + k + 1)
                    act.wait_ge(q_copied, q_job(b, k))
                    nc.scalar.copy(v[b][:, HI, 2 * k:2 * k + 2, :], q_raw[:, k % 2, :, 1, :]).then_inc(v_hi_ready, 1)
                for c in range(CH):
                    t_hi(kT[b][:, HI, chunk(c)], 6 * b + 4 + c + 1)
            for k in range(4):
                q_copy(2, k, 6 * B + k + 1)
            for c in range(CH):
                t_hi(qT[:, 0, HI, chunk(c)], 6 * B + 4 + c + 1)

            def o_hi(head, free):
                act.wait_ge(pv_done, NT * (head + 1))
                if free:
                    act.wait_ge(y_job_ready, y_job(head - 1, 4))
                nc.scalar.copy(oT[:, HI, :].rearrange("p (c n) -> p c n", c=CH), pO[:, :, :]).then_inc(o_hi_ready, 1)

            def between(slot):
                for g in range(GROUPS):
                    stage = slot - BETWEEN[g]
                    if stage == NORMALISE_1:
                        if g:
                            act.wait_ge(x_job_ready, between_job(g - 1, 1))
                        normalise(ln_third(g), resid[:, GT * g:GT * g + GT, :])
                    if stage == NORMALISE_2:
                        normalise(ln_third(g) + 1, resid[:, GT * g:GT * g + GT, :])
                    if stage in TRANSPOSE_AT:
                        k, c = TRANSPOSE_AT.index(stage), g % 2
                        t_hi(xT[g // 2][:, HI, k, chunk(c)], between_job(g, k))
                    if stage == ROUTE_EXP:
                        act.wait_ge(top_ready, g + 1)
                        nc.scalar.activation(r_e[:, :], r_d[:, :], ACT.Exp).then_inc(exp_ready, 1)
                    if stage == ROUTE_T:
                        act.wait_ge(x_job_ready, between_job(g, 4))
                        if g:
                            act.wait_ge(x_bank_free, between_job(g - 1, 4))
                        nc.scalar.copy(rT_hi[:, :], pX[0:2 * E, :]).then_inc(rT_hi_ready, 1)

            def split_hi(t):
                act.wait_ge(e_raw_in[t % 2], 16 * (t // 2 + 1))
                nc.scalar.copy(expert_w[:, t, HI, :], e_raw[:, t % 2, :]).then_inc(ehi_ready, 1)

            def steps(it, b, first, last):
                start, end = b == 0 and first, b == B - 1 and last
                for s in range(STEPS):
                    t = step(it, s)
                    act.wait_ge(scores_ready, t + 1)
                    if not (start and s < 4):
                        act.wait_ge(pv_done, t - 3)
                    nc.scalar.activation(phi[:, s % 4, :].rearrange("p (c n) -> p c n", c=CH), pS[:, s % 2, :, :],
                                         ACT.Exp, scale=16.0).then_inc(phi_ready, 1)
                    if not (start and s < 4):
                        act.wait_ge(psum_added, added(it, s - 4))
                    nc.scalar.activation(p32[:, s % 4, :].rearrange("p (c n) -> p c n", c=CH), pS[:, s % 2, :, :],
                                         ACT.Exp, scale=16.0).then_inc(p32_ready, 1)
                    if s in B_AT:
                        c = B_AT.index(s)
                        t_hi(qT[:, 1, HI, chunk(c)], x_job(it, c))
                    if s in Q_AT and not end:
                        q_copy(it + 3, Q_AT.index(s), x_job(it, 2 + Q_AT.index(s)))
                    if s in A_AT and not end:
                        c = A_AT.index(s)
                        t_hi(qT[:, 0, HI, chunk(c)], x_job(it, 6 + c))
                    if s == 0 and not start:
                        o_hi(2 * it - 1, True)
                    if s == NT:
                        o_hi(2 * it, not start)
                    if end:
                        between(s)

            act.wait_ge(dma_scratch, 16 * 8)
            iterations(act, steps)
            o_hi(2 * ITERS - 1, True)

            act.wait_ge(psum_added, 7 * 2 * ITERS)
            for t in range(AHEAD):
                split_hi(t)
            for n in range(GROUPS * RT):
                act.wait_ge(gu_ready, n + 1)
                if n >= 2:
                    act.wait_ge(u_done, n - 1)
                nc.scalar.activation(act_s[:, n % 2, :], pS[:, n % 2, 0, :], ACT.Silu).then_inc(silu_done, 1)
                act.wait_ge(a_done, n + 1)
                if n >= 2:
                    act.wait_ge(down_done, n - 1)
                nc.scalar.copy(act_hi[:, n % 2, :], act_a[:, n % 2, :]).then_inc(ahi_done, 1)
                if n + AHEAD < RT:
                    split_hi(n + AHEAD)
                between(STEPS + n)

        @block.vector
        def _(dve):
            dve.wait_ge(cond_exp, 1)
            nc.vector.tensor_scalar(cond_e[:, :, :], cond_e[:, :, :], 1.0, None, ALU.add).then_inc(cond_den, 1)
            dve.wait_ge(cond_den, 1)
            nc.vector.reciprocal(cond_e[:, :, :], cond_e[:, :, :]).then_inc(cond_den, 1)
            dve.wait_ge(cond_den, 2)
            nc.vector.tensor_tensor(condT[:, :, :], condT[:, :, :], cond_e[:, :, :], ALU.mult).then_inc(cond_den, 1)
            dve.wait_ge(cond_den, 3)
            nc.vector.tensor_copy(silu_rows[:, :, :, :], condT[:, :, :].unsqueeze(3).broadcast_to([P, KC, B, P])).then_inc(silu_ready, 1)

            def ln(n, src, count=None):
                for t in range(GT):
                    ins = nc.vector.bn_stats(ln_stats[:, n, t, :], src[:, t, :])
                ins.then_inc(ln_sem, 1)
                dve.wait_ge(ln_sem, n + 1)
                for t in range(GT):
                    ins = nc.vector.bn_aggr(ln_mv[:, n, t, :], ln_stats[:, n, t, :])
                ins.then_inc(stats_ready, 1)

            def rows(b, which):
                return mod[:, b, which, :].unsqueeze(1).broadcast_to([P, GT, D])

            def transposed_lo(i, b, c):
                for k in range(KC):
                    dve.wait_ge(xt_hi_ready, KC * i + k + 1)
                    nc.vector.tensor_tensor(xT[b][:, LO, k, c * BANK:(c + 1) * BANK], pS[:, 0, k, :],
                                            xT[b][:, HI, k, c * BANK:(c + 1) * BANK], ALU.subtract).then_inc(xt_lo_ready, 1)

            def modulate(b, half_rows, count, normed_count):
                dve.wait_ge(normed, normed_count)
                nc.vector.tensor_tensor(z[:, :, :], z[:, :, :], rows(b, half_rows + SCALE), ALU.mult).then_inc(modulated, 1)
                dve.wait_ge(modulated, count)
                nc.vector.tensor_tensor(z[:, :, :], z[:, :, :], rows(b, half_rows + SHIFT), ALU.add).then_inc(modulated, 1)
                dve.wait_ge(modulated, count + 1)

            dve.wait_ge(router_hi, 1)
            nc.vector.tensor_tensor(router_sb[:, LO, :, :], router_raw[:, :, :], router_sb[:, HI, :, :], ALU.subtract).then_inc(router_lo, 1)
            for g in range(GROUPS):
                dve.wait_ge(dma_x[g], 16)
                ln(ln_first(g), resid[:, GT * g:GT * g + GT, :])
                if g == 0:
                    dve.wait_ge(mod_copied, 2 * 3)
                    for h in (0, 3):
                        nc.vector.tensor_scalar(mod[:, :, h + SCALE, :], mod[:, :, h + SCALE, :], 1.0, None, ALU.add).then_inc(mod_done, 1)
                    dve.wait_ge(mod_done, 2)
                modulate(g // 2, 0, 2 * g + 1, 2 * GT * g + GT)
                ln(ln_first(g) + 1, z)
                transposed_lo(g, g // 2, g % 2)
                if g == 0:
                    for k in range(KC):
                        dve.wait_ge(whi_ready, k + 1)
                        nc.vector.scalar_tensor_tensor(out=wkv_sb[:, LO, k, :], in0=wkv_raw[:, k, :], scalar=gnorm[:, k:k + 1],
                                                       in1=wkv_sb[:, HI, k, :], op0=ALU.mult, op1=ALU.subtract).then_inc(wlo_ready, 1)
                    for k in range(KC):
                        dve.wait_ge(whi_ready, KC + k + 1)
                        view = [w[:, :, :].rearrange("p (n a) f -> p a n f", a=2)[:, k] for w in (w_hi, w_lo)]
                        nc.vector.scalar_tensor_tensor(out=view[LO], in0=w_raw[:, k, :].rearrange("p (n f) -> p n f", f=D),
                                                       scalar=gnorm[:, k:k + 1], in1=view[HI], op0=ALU.mult, op1=ALU.subtract).then_inc(wlo_ready, 1)
            for i, h in enumerate((GATE, 3 + GATE)):
                nc.vector.tensor_scalar(gate_sign[:, :, :], mod[:, :, h, :], 0.0, 2.0, ALU.is_ge, ALU.mult).then_inc(mod_done, 1)
                nc.vector.scalar_tensor_tensor(out=mod[:, :, h, :], in0=mod[:, :, h, :], scalar=-1.0, in1=mod[:, :, h, :],
                                               op0=ALU.mult, op1=ALU.max).then_inc(mod_done, 1)
                dve.wait_ge(mod_done, 4 * i + 4)
                nc.vector.tensor_scalar(mod[:, :, h, :], mod[:, :, h, :], 0.25, None, ALU.max).then_inc(mod_done, 1)
                dve.wait_ge(mod_done, 4 * i + 5)
                nc.vector.scalar_tensor_tensor(out=mod[:, :, h, :], in0=gate_sign[:, :, :], scalar=-1.0, in1=mod[:, :, h, :],
                                               op0=ALU.add, op1=ALU.mult).then_inc(mod_done, 1)
                dve.wait_ge(mod_done, 4 * i + 6)
            nc.vector.tensor_tensor(mod[:, :, GATE, :], mod[:, :, GATE, :], gout[:, :].unsqueeze(1).broadcast_to([P, B, D]), ALU.mult).then_inc(mod_done, 1)
            dve.wait_ge(whi_ready, KC + 3)
            nc.vector.tensor_tensor(w_lo[:, :, :].rearrange("p h f -> p (h f)"), w_raw[:, :, :].rearrange("p k n -> p (k n)"),
                                    w_hi[:, :, :].rearrange("p h f -> p (h f)"), ALU.subtract).then_inc(wlo_ready, 1)

            def chunk(c):
                return slice(c * BANK, (c + 1) * BANK)

            def q_scale(n, k, bank_job):
                dve.wait_ge(x_bank_free, bank_job)
                if not (isinstance(n, int) and n == 0 and k == 0):
                    dve.wait_ge(q_rn_ready, q_job(n, k) - 1)
                nc.vector.tensor_reduce(q_ss[:, :], q_sq[:, :, :, :].rearrange("p t h d -> p (t h) d"), AX.X, ALU.add).then_inc(q_ss_ready, 1)

            def q_apply(n, k):
                dve.wait_ge(q_rn_ready, q_job(n, k))
                nc.vector.tensor_tensor(qn[:, 2 * k:2 * k + 2, :, :].rearrange("p t h d -> p (t h) d"),
                                        q_raw[:, k % 2, :, :, :].rearrange("p t h d -> p (t h) d"),
                                        q_rn[:, k % 2, :].unsqueeze(2).broadcast_to([P, 4, DH]), ALU.mult).then_inc(qn_ready, 1)

            def t_lo(hi, dst, count):
                dve.wait_ge(t_hi_ready, count)
                nc.vector.tensor_tensor(dst, pX[:, :], hi, ALU.subtract).then_inc(x_bank_free, 1)

            for b in range(B):
                for k in range(4):
                    q_scale(b, k, 6 * b + k + 1)
                    dve.wait_ge(v_hi_ready, 4 * b + k + 1)
                    nc.vector.tensor_tensor(v[b][:, LO, 2 * k:2 * k + 2, :], q_raw[:, k % 2, :, 1, :],
                                            v[b][:, HI, 2 * k:2 * k + 2, :], ALU.subtract).then_inc(v_lo_ready, 1)
                    q_apply(b, k)
                for c in range(CH):
                    t_lo(kT[b][:, HI, chunk(c)], kT[b][:, LO, chunk(c)], 2 * b + c + 1)
            for k in range(4):
                q_scale(2, k, 6 * B + k + 1)
                q_apply(2, k)
            for c in range(CH):
                t_lo(qT[:, 0, HI, chunk(c)], qT[:, 0, LO, chunk(c)], t_job(0, c))

            def o_lo(head):
                dve.wait_ge(o_hi_ready, head + 1)
                nc.vector.tensor_tensor(oT[:, LO, :].rearrange("p (c n) -> p c n", c=CH), pO[:, :, :],
                                        oT[:, HI, :].rearrange("p (c n) -> p c n", c=CH), ALU.subtract).then_inc(o_lo_ready, 1)

            def row_sums(head, parity):
                dve.wait_ge(y_job_ready, y_job(head, 0))
                nc.vector.reciprocal(rz[:, parity, :], pY[:, 0:NT]).then_inc(y_bank_free, 1)

            def add_head(head, k, parity, b, new):
                dve.wait_ge(y_job_ready, y_job(head, k + 1))
                dve.wait_ge(y_bank_free, y_job(head, 0))
                for i in range(2):
                    t = 2 * k + i
                    dst = resid[:, NT * b + t, :]
                    src = pY[:, i * D:(i + 1) * D]
                    if new:
                        ins = nc.vector.tensor_scalar(dst, src, rz[:, parity, t:t + 1], None, ALU.mult)
                    else:
                        ins = nc.vector.scalar_tensor_tensor(out=dst, in0=src, scalar=rz[:, parity, t:t + 1], in1=dst,
                                                             op0=ALU.mult, op1=ALU.add)
                ins.then_inc(y_bank_free, 1)

            chain = [0]

            def link(ins):
                chain[0] += 1
                ins.then_inc(route_chain, 1)
                dve.wait_ge(route_chain, chain[0])

            def between(slot):
                for g in range(GROUPS):
                    stage = slot - BETWEEN[g]
                    b, m = g // 2, 2 * GROUPS + 4 * g
                    here = resid[:, GT * g:GT * g + GT, :]
                    if stage == STATS_1:
                        dve.wait_ge(y_bank_free, y_job(HEADS * (b + 1) - 1, 4))
                        ln(ln_third(g), here)
                    if stage == GATE_ADD:
                        dve.wait_ge(normed, 2 * GT * GROUPS + 2 * GT * g + GT)
                        nc.vector.tensor_tensor(z[:, :, :], z[:, :, :], rows(b, GATE), ALU.mult).then_inc(modulated, 1)
                        dve.wait_ge(modulated, m + 1)
                        dve.wait_ge(x_again_in, 16 * (g + 1))
                        nc.vector.tensor_tensor(here, z[:, :, :], x_again[:, :, :], ALU.add).then_inc(modulated, 1)
                        dve.wait_ge(modulated, m + 2)
                        ln(ln_third(g) + 1, here)
                    if stage == MODULATE:
                        modulate(b, 3, m + 3, 2 * GT * GROUPS + 2 * GT * g + 2 * GT)
                    if stage in TRANSPOSE_AT:
                        k, c = TRANSPOSE_AT.index(stage), g % 2
                        t_lo(xT[b][:, HI, k, chunk(c)], xT[b][:, LO, k, chunk(c)], t_job(ITERS, KC * g + k))
                    if stage == LOGITS:
                        dve.wait_ge(x_job_ready, between_job(g, 2))
                        nc.vector.tensor_copy(logits_T[:, :], pX[0:E, :]).then_inc(x_bank_free, 1)
                    if stage == LOGITS_T:
                        dve.wait_ge(x_job_ready, between_job(g, 3))
                        nc.vector.tensor_copy(logits[:, :, :], pX[:, 0:GT * E].rearrange("p (t e) -> p t e", e=E)).then_inc(x_bank_free, 1)
                        dve.wait_ge(x_bank_free, between_job(g, 3))
                        for t in range(GT):
                            ins = nc.vector.max(top[:, t, :], logits[:, t, :])
                        link(ins)
                        for t in range(GT):
                            ins = nc.vector.max_index(top_at[:, t, :], top[:, t, :], logits[:, t, :])
                        link(ins)
                        link(nc.vector.tensor_copy(top_f[:, :, :], top_at[:, :, 0:TOPK]))
                        nc.vector.tensor_tensor(r_d[:, :], top[:, :, 1], top[:, :, 0], ALU.subtract).then_inc(top_ready, 1)
                    if stage == ROUTE_EXP:
                        dve.wait_ge(exp_ready, g + 1)
                        link(nc.vector.tensor_scalar(r_den[:, :], r_e[:, :], 1.0, None, ALU.add))
                        link(nc.vector.reciprocal(r_w[:, :, 0], r_den[:, :]))
                        link(nc.vector.tensor_tensor(r_w[:, :, 1], r_w[:, :, 0], r_e[:, :], ALU.mult))
                        for t in range(GT):
                            nc.vector.tensor_scalar(r_one[:, t, :], experts, top_f[:, t, 0:1], r_w[:, t, 0:1], ALU.is_equal, ALU.mult)
                            ins = nc.vector.tensor_scalar(r_two[:, t, :], experts, top_f[:, t, 1:2], r_w[:, t, 1:2], ALU.is_equal, ALU.mult)
                        link(ins)
                        if g:
                            dve.wait_ge(x_job_ready, between_job(g - 1, 4))
                        nc.vector.tensor_tensor(route[:, :, 0:E], r_one[:, :, :], r_two[:, :, :], ALU.add)
                        nc.vector.tensor_tensor(route[:, :, E:2 * E], r_one[:, :, :], r_two[:, :, :], ALU.add).then_inc(route_ready, 1)
                    if stage == ROUTE_T:
                        dve.wait_ge(rT_hi_ready, g + 1)
                        if g >= 2:
                            dve.wait_ge(cw_ready, RT * (g - 1))
                        nc.vector.scalar_tensor_tensor(out=rT[:, g % 2, :], in0=rT_hi[:, :], scalar=small[0:2 * E, P:P + 1],
                                                       in1=pX[0:2 * E, :], op0=ALU.mult, op1=ALU.add).then_inc(x_bank_free, 1)

            def split_lo(t):
                dve.wait_ge(ehi_ready, t + 1)
                nc.vector.tensor_tensor(expert_w[:, t, LO, :], e_raw[:, t % 2, :], expert_w[:, t, HI, :], ALU.subtract).then_inc(elo_ready, 1)

            def steps(it, b, first, last):
                start, end = b == 0 and first, b == B - 1 and last
                before_b = b - 1 if first else b
                for s in range(STEPS):
                    t, head, j = step(it, s), 2 * it + s // NT, s % NT
                    dve.wait_ge(p32_ready, t + 1)
                    if not (start and s < 2):
                        dve.wait_ge(pv_done, t - 1)
                    nc.vector.tensor_tensor(plo[:, s % 2, :], p32[:, s % 4, :], phi[:, s % 4, :], ALU.subtract).then_inc(plo_ready, 1)
                    if j:
                        total = psums[:, (s // NT) % 2, :]
                        if j == 1 and not start:
                            dve.wait_ge(y_job_ready, y_job(head - 2, 0))
                        if j > 1:
                            dve.wait_ge(psum_added, 7 * head + j - 1)
                        nc.vector.tensor_tensor(total, p32[:, (s - 1) % 4, :] if j == 1 else total, p32[:, s % 4, :], ALU.add).then_inc(psum_added, 1)
                    if s in B_AT:
                        c = B_AT.index(s)
                        t_lo(qT[:, 1, HI, chunk(c)], qT[:, 1, LO, chunk(c)], t_job(it, 2 + c))
                    if not end:
                        if s in Q_AT:
                            q_scale(it + 3, Q_AT.index(s), x_job(it, 2 + Q_AT.index(s)))
                        if s - 1 in Q_AT:
                            q_apply(it + 3, Q_AT.index(s - 1))
                        if s in A_AT:
                            c = A_AT.index(s)
                            t_lo(qT[:, 0, HI, chunk(c)], qT[:, 0, LO, chunk(c)], t_job(it + 1, c))
                    if not start:
                        if s == Z_B:
                            row_sums(2 * it - 1, 1)
                        if s in OB_AT:
                            add_head(2 * it - 1, OB_AT.index(s), 1, before_b, False)
                    if s == Z_A:
                        row_sums(2 * it, 0)
                    if s in OA_AT:
                        add_head(2 * it, OA_AT.index(s), 0, b, first)
                    if s == 0 and not start:
                        o_lo(2 * it - 1)
                    if s == NT:
                        o_lo(2 * it)
                    if end:
                        between(s)

            dve.wait_ge(dma_scratch, 16 * 8)
            iterations(dve, steps)
            o_lo(2 * ITERS - 1)
            split_lo(0)
            row_sums(2 * ITERS - 1, 1)
            for k in range(4):
                add_head(2 * ITERS - 1, k, 1, B - 1, False)
                if k == 1:
                    split_lo(1)
            for t in range(2, AHEAD):
                split_lo(t)

            def output(g):
                dve.wait_ge(down_done, RT * (g + 1))
                if g:
                    dve.wait_ge(dma_out, 16 * g)
                nc.vector.tensor_tensor(o_sb[:, :, :], pO[:, :, :].rearrange("p c (t f) -> p (c t) f", f=D), rows(g // 2, 3 + GATE), ALU.mult).then_inc(o_mul, 1)
                dve.wait_ge(o_mul, g + 1)
                nc.vector.tensor_tensor(o_sb[:, :, :], o_sb[:, :, :], resid[:, GT * g:GT * g + GT, :], ALU.add).then_inc(o_done, 1)

            for n in range(GROUPS * RT):
                dve.wait_ge(silu_done, n + 1)
                if n:
                    dve.wait_ge(a_done, n)
                nc.vector.tensor_tensor(act_u[:, :], act_s[:, n % 2, :], pS[:, n % 2, 1, :], ALU.mult).then_inc(u_done, 1)
                dve.wait_ge(u_done, n + 1)
                dve.wait_ge(cw_ready, n + 1)
                if n >= 2:
                    dve.wait_ge(ahi_done, n - 1)
                nc.vector.tensor_tensor(act_a[:, n % 2, :], act_u[:, :], pY[:, :], ALU.mult).then_inc(a_done, 1)
                if n and n % RT == 0:
                    output(n // RT - 1)
                if n + AHEAD < RT:
                    split_lo(n + AHEAD)
                dve.wait_ge(ahi_done, n + 1)
                nc.vector.tensor_tensor(act_lo[:, n % 2, :], act_a[:, n % 2, :], act_hi[:, n % 2, :], ALU.subtract).then_inc(alo_done, 1)
                between(STEPS + n)
            output(GROUPS - 1)

        @block.tensor
        def _(pe):
            pe.wait_ge(silu_ready, 1)
            pe.wait_ge(dma_wmod, 16)
            for c in range(3):
                for b in range(B):
                    i = B * c + b
                    dst = pS[:, i // 2, i % 2, :] if i < 4 else pO[:, i % 2, :]
                    for k in range(KC):
                        mm = pe.matmul(dst, silu_rows[:, k, b, :], wmod_sb[:, k, c * BANK:(c + 1) * BANK], start=(k == 0), stop=(k == KC - 1))
                    mm.then_inc(mod_ready, 1)
            pe.wait_ge(dma_const, 16 * 3)

            def transpose_group(i):
                for k in range(KC):
                    if i:
                        pe.wait_ge(xt_lo_ready, KC * (i - 1) + k + 1)
                    for t in range(GT):
                        mm = pe.transpose(pS[:, 0, k, t * P:(t + 1) * P], z[:, t, k * P:(k + 1) * P], ident)
                    mm.then_inc(xt_ready, 1)

            pe.wait_ge(mod_copied, 6)
            for g in range(GROUPS):
                pe.wait_ge(normed, 2 * GT * (g + 1))
                transpose_group(g)

            def project(n, k, b, w, job, free):
                if free:
                    pe.wait_ge(x_bank_free, job - 1)
                for i in range(2):
                    t = 2 * k + i
                    for p, (s, m) in enumerate(PASSES):
                        for c in range(KC):
                            mm = pe.matmul(pX[:, i * D:(i + 1) * D], xT[b][:, s, c, t * P:(t + 1) * P], w[:, m, c, :],
                                           start=(p == 0 and c == 0), stop=(p == 2 and c == KC - 1))
                mm.then_inc(x_job_ready, 1)

            def transpose_head(h, c, job):
                pe.wait_ge(x_bank_free, job - 1)
                for i in range(GT):
                    mm = pe.transpose(pX[:, i * P:(i + 1) * P], qn[:, GT * c + i, h, :], ident)
                mm.then_inc(x_job_ready, 1)

            pe.wait_ge(wlo_ready, KC)
            for b in range(B):
                pe.wait_ge(xt_lo_ready, 2 * KC * (b + 1))
                for k in range(4):
                    project(b, k, b, wkv_sb, 6 * b + k + 1, b or k)
                pe.wait_ge(qn_ready, q_job(b, 3))
                for c in range(CH):
                    transpose_head(0, c, 6 * b + 4 + c + 1)
            pe.wait_ge(wq_in, 16)
            for k in range(4):
                project(2, k, 0, wq_sb, 6 * B + k + 1, True)
            pe.wait_ge(qn_ready, q_job(2, 3))
            for c in range(CH):
                transpose_head(0, c, 6 * B + 4 + c + 1)

            def scores(b, s):
                h, j = (s // NT) % 2, s % NT
                for p, (a, m) in enumerate(PASSES):
                    for c in range(CH):
                        mm = pe.matmul(pS[:, s % 2, c, :], kT[b][:, a, j * P:(j + 1) * P], qT[:, h, m, c * BANK:(c + 1) * BANK],
                                       start=(p == 0), stop=(p == 2))
                mm.then_inc(scores_ready, 1)

            def weighted_values(it, b, s, fresh):
                j = s % NT
                pe.wait_ge(phi_ready, step(it, s) + 1)
                if j == 0 and not fresh:
                    pe.wait_ge(o_lo_ready, 2 * it + s // NT)
                for p, (a, m) in enumerate(((LO, HI), (HI, HI), (HI, LO))):
                    if m == LO:
                        pe.wait_ge(plo_ready, step(it, s) + 1)
                    moving = phi[:, s % 4, :] if m == HI else plo[:, s % 2, :]
                    for c in range(CH):
                        mm = pe.matmul(pO[:, c, :], v[b][:, a, j, :], moving[:, c * BANK:(c + 1) * BANK],
                                       start=(j == 0 and p == 0), stop=(j == NT - 1 and p == 2))
                mm.then_inc(pv_done, 1)

            def sums(head, parity, free):
                pe.wait_ge(psum_added, 7 * (head + 1))
                if free:
                    pe.wait_ge(y_bank_free, y_job(head - 1, 4))
                for t in range(NT):
                    mm = pe.matmul(pY[:, t:t + 1], psums[:, parity, t * P:(t + 1) * P], ones[:, :], start=True, stop=True)
                mm.then_inc(y_job_ready, 1)

            def project_out(head, k, parity, landed, count):
                pe.wait_ge(y_bank_free, y_job(head, k))
                if k == 0:
                    pe.wait_ge(o_lo_ready, head + 1)
                    pe.wait_ge(landed, count)
                for i in range(2):
                    t = 2 * k + i
                    for p, (a, m) in enumerate(PASSES):
                        mm = pe.matmul(pY[:, i * D:(i + 1) * D], oT[:, a, t * P:(t + 1) * P], wout_sb[parity][:, m, :], start=(p == 0), stop=(p == 2))
                mm.then_inc(y_job_ready, 1)

            pe.wait_ge(x_bank_free, 6 * B + 6)
            scores(0, 0)

            def between(slot):
                for g in range(GROUPS):
                    stage = slot - BETWEEN[g]
                    if stage in TRANSPOSE_AT:
                        k = TRANSPOSE_AT.index(stage)
                        pe.wait_ge(modulated, 2 * GROUPS + 4 * g + 4)
                        pe.wait_ge(x_bank_free, between_job(g, k) - 1)
                        for t in range(GT):
                            mm = pe.transpose(pX[:, t * P:(t + 1) * P], z[:, t, k * P:(k + 1) * P], ident)
                        mm.then_inc(x_job_ready, 1)
                    if stage == LOGITS:
                        pe.wait_ge(x_bank_free, between_job(g, 1))
                        pe.wait_ge(router_lo, 1)
                        for p, (a, m) in enumerate(PASSES):
                            for c in range(KC):
                                mm = pe.matmul(pX[0:E, :], router_sb[:, a, c, :], xT[g // 2][:, m, c, (g % 2) * BANK:(g % 2 + 1) * BANK],
                                               start=(p == 0 and c == 0), stop=(p == 2 and c == KC - 1))
                        mm.then_inc(x_job_ready, 1)
                    if stage == LOGITS_T:
                        pe.wait_ge(x_bank_free, between_job(g, 2))
                        for t in range(GT):
                            mm = pe.transpose(pX[:, t * E:(t + 1) * E], logits_T[:, t * P:(t + 1) * P], ident[0:E, 0:E])
                        mm.then_inc(x_job_ready, 1)
                    if stage == ROUTE_T:
                        pe.wait_ge(route_ready, g + 1)
                        pe.wait_ge(x_bank_free, between_job(g, 3))
                        for t in range(GT):
                            mm = pe.transpose(pX[0:2 * E, t * P:(t + 1) * P], route[:, t, :], ident)
                        mm.then_inc(x_job_ready, 1)

            def up(n, parts=(0, 1)):
                g, t = n // RT, n % RT
                if n >= 2:
                    pe.wait_ge(u_done, n - 1)
                if g == 0:
                    pe.wait_ge(elo_ready, t + 1)
                if t == 0:
                    pe.wait_ge(x_bank_free, between_job(g, 1))
                for u in parts:
                    for p, (a, m) in enumerate(PASSES):
                        for c in range(KC):
                            at = (KC * u + c) * P
                            mm = pe.matmul(pS[:, n % 2, u, :], expert_w[:, t, a, at:at + P],
                                           xT[g // 2][:, m, c, (g % 2) * BANK:(g % 2 + 1) * BANK],
                                           start=(p == 0 and c == 0), stop=(p == 2 and c == KC - 1))
                if parts[-1] == 1:
                    mm.then_inc(gu_ready, 1)

            def routing(n):
                g, t = n // RT, n % RT
                if t == 0:
                    pe.wait_ge(x_bank_free, between_job(g, 4))
                if n:
                    pe.wait_ge(a_done, n)
                else:
                    pe.wait_ge(select_in, 16)
                    pe.wait_ge(y_bank_free, y_job(2 * ITERS - 1, 4))
                pe.matmul(pY[:, :], select[:, t * P:(t + 1) * P], rT[:, g % 2, :], start=True, stop=True).then_inc(cw_ready, 1)

            def down(n):
                g, t = n // RT, n % RT
                pe.wait_ge(alo_done, n + 1)
                if t == 0 and g:
                    pe.wait_ge(o_mul, g)
                for i in range(GT):
                    for p, (a, m) in enumerate(PASSES):
                        w = (act_hi, act_lo)[a][:, n % 2, i * P:(i + 1) * P]
                        mm = pe.matmul(pO[:, i // 2, (i % 2) * D:(i % 2 + 1) * D], w, expert_w[:, t, m, 2 * KC * P:TILE],
                                       start=(t == 0 and p == 0 and i % 2 == 0), stop=(t == RT - 1 and p == 2), skip_group_check=True)
                mm.then_inc(down_done, 1)

            def steps(it, b, first, last):
                start, end = b == 0 and first, b == B - 1 and last
                q_batch = b + 1 if last else b
                for s in range(STEPS):
                    if not (end and s == STEPS - 1):
                        if not (start and s == 0):
                            pe.wait_ge(p32_ready, step(it, s))
                        if s == NT - 1:
                            pe.wait_ge(x_bank_free, x_job(it, 1))
                        if s == STEPS - 1:
                            pe.wait_ge(x_bank_free, x_job(it, 7))
                        scores(q_batch if s == STEPS - 1 else b, s + 1)
                    if s in B_AT:
                        transpose_head(1, B_AT.index(s), x_job(it, B_AT.index(s)))
                    if not end:
                        if s in Q_AT:
                            k = Q_AT.index(s)
                            if k == 0:
                                pe.wait_ge(wq_in, 16 * (it + 2))
                            project(it + 3, k, q_batch, wq_sb, x_job(it, 2 + k), True)
                        if s in A_AT:
                            if s == A_AT[0]:
                                pe.wait_ge(qn_ready, q_job(it + 3, 3))
                            transpose_head(0, A_AT.index(s), x_job(it, 6 + A_AT.index(s)))
                    if not start:
                        if s == Z_B:
                            sums(2 * it - 1, 1, True)
                        if s in OB_AT:
                            project_out(2 * it - 1, OB_AT.index(s), 1, woutb_in, 16 * it)
                    if s == Z_A:
                        sums(2 * it, 0, not start)
                    if s in OA_AT:
                        project_out(2 * it, OA_AT.index(s), 0, wouta_in, 16 * (it + 1))
                    if s:
                        weighted_values(it, b, s - 1, start and s == 1)
                    elif not start:
                        weighted_values(it - 1, b - 1 if first else b, STEPS - 1, False)
                    if end:
                        between(s)

            iterations(pe, steps)
            weighted_values(ITERS - 1, B - 1, STEPS - 1, False)
            sums(2 * ITERS - 1, 1, True)
            for k in range(4):
                project_out(2 * ITERS - 1, k, 1, woutb_in, 16 * ITERS)
                if k == 0:
                    pe.wait_ge(p32_ready, STEPS * ITERS)
                up(k // 2, (k % 2,))
            routing(0)

            for n in range(GROUPS * RT):
                if n + 1 < GROUPS * RT:
                    routing(n + 1)
                between(STEPS + n)
                if n + 2 < GROUPS * RT:
                    up(n + 2)
                down(n)


B_AT = [0, 2]
Q_AT = [3, 5, 7, 9]
A_AT = [12, 13]
Z_B, Z_A = 1, 10
OB_AT = [2, 3, 4, 6]
OA_AT = [11, 12, 13, 14]


STATS_1, NORMALISE_1, GATE_ADD, NORMALISE_2, MODULATE = 0, 2, 3, 5, 6
TRANSPOSE_AT = (7, 8)
LOGITS, LOGITS_T, ROUTE_EXP, ROUTE_T = 9, 10, 11, 12
BETWEEN = (1, 12, 23, 34)
AHEAD = 3


def row_tiles(w1, w2):
    def stationary(w):
        return w.reshape(RT, P, KC, P).transpose(0, 3, 2, 1).reshape(RT, P, KC * P)
    down = w2.transpose(0, 2, 1).reshape(RT, P, D)
    return np.concatenate([stationary(w1[:, :INNER]), stationary(w1[:, INNER:]), down], axis=2)


def kernel(**inputs):
    import concourse.bacc as bacc
    from concourse.bass_utils import run_bass_kernel_spmd

    laid_out = {
        "x": np.asarray(inputs["L0_attn_x"]),
        "g_norm": np.asarray(inputs["L0_attn_g_norm"]).reshape(KC, P).T,
        "wq": np.asarray(inputs["L0_attn_Wq"]),
        "wkv": np.asarray(inputs["L0_attn_Wkv"]),
        "wout": np.asarray(inputs["L0_attn_Wout"]),
        "g_out": np.asarray(inputs["L0_attn_g_out"]),
        "router": np.asarray(inputs["L0_ffn_router_w"]).T,
        "experts_w": row_tiles(np.asarray(inputs["L0_ffn_w1"]), np.asarray(inputs["L0_ffn_w2"])),
        "cond": np.asarray(inputs["L0_c"]).T.reshape(KC, P, B).transpose(1, 0, 2),
        "wmod": np.asarray(inputs["L0_wmod"]),
        "consts": shape_constants(),
    }
    nc = bacc.Bacc("TRN2", target_bir_lowering=False, num_devices=1)
    arrays, args = {}, []
    for name, a in laid_out.items():
        a = np.ascontiguousarray(a)
        arrays[f"in_{name}"] = a
        args.append(nc.dram_tensor(f"in_{name}", a.shape, mybir.dt.from_np(a.dtype), kind="ExternalInput").ap())
    args.append(nc.dram_tensor("out_x", (B, N, D), F32, kind="ExternalOutput").ap())
    adaln_block(nc, *args)
    return run_bass_kernel_spmd(nc, [arrays], core_ids=[0]).results[0]["out_x"]
```

```python
from contextlib import ExitStack

import numpy as np

import concourse.bass as bass
from concourse import mybir

P = 128
BANK = 512
B, N, D = 2, 1024, 256
EPS_LN = 1e-5
EPS_Q = 1e-12 / 256.0
EPS_K = 1e-12
POOL_CONSTANTS = (-0.5, 1.5, EPS_LN, EPS_K, EPS_Q)
KC = D // P
HEADS, DH = 16, 128
PAIRS = HEADS // 2
NT = N // P
CH = N // BANK
STEPS = 2 * NT
ITERS = B * PAIRS
E, TOPK, INNER = 8, 2, 176
ROWS = E * INNER
RT = ROWS // P
GROUPS = B * N // BANK
GT = BANK // P
TILE = 2 * KC * P + D
SMALL = P + 1 + E
SHIFT, SCALE, GATE = 0, 1, 2

F32 = mybir.dt.float32
F32R = mybir.dt.float32r
U32 = mybir.dt.uint32
ALU = mybir.AluOpType
ACT = mybir.ActivationFunctionType
AX = mybir.AxisListType

HI, LO = 0, 1
PASSES = ((LO, HI), (HI, HI), (HI, LO))


def shape_constants():
    select = np.zeros((P, ROWS), np.float32)
    for k in range(2 * E):
        select[k, (k % E) * INNER:(k % E + 1) * INNER] = 1.0
    not_hi = np.zeros((P, 1), np.float32)
    not_hi[E:2 * E] = -1.0
    experts = np.tile(np.arange(E, dtype=np.float32), (P, 1))
    return np.concatenate([np.eye(P, dtype=np.float32), not_hi, experts, select], axis=1)


def adaln_block(nc, x, g_norm, wq, wkv, wout, g_out, router, experts_w, cond, wmod,
                consts, out):
    ctx = ExitStack()
    with ctx:
        def sb(name, shape, dt=F32, where=ctx):
            return where.enter_context(nc.sbuf_tensor(name, shape, dt))

        def sem(name):
            return ctx.enter_context(nc.semaphore(name))

        small = sb("small", [P, SMALL])
        ident = small[:, 0:P]
        experts = small[:, P + 1:SMALL]
        ones = sb("ones", [P, 1])
        mod = sb("mod", [P, B, 6, D])
        gnorm = sb("gnorm", [P, KC])
        condT = sb("condT", [P, KC, B])
        cond_e = sb("cond_e", [P, KC, B])
        resid = sb("resid", [P, B * NT, D])
        xT = [sb(f"xT{b}", [P, 2, KC, N], F32R) for b in range(B)]
        LNS = 4 * GROUPS
        ln_stats = sb("ln_stats", [P, LNS, GT, 6])
        ln_mv = sb("ln_mv", [P, LNS, GT, 2])
        ln_r = sb("ln_r", [P, LNS, GT])
        ln_nb = sb("ln_nb", [P, LNS, GT])
        ln_t = sb("ln_t", [P, 3, GT])
        pool_c = sb("pool_c", [P, len(POOL_CONSTANTS), 2 * NT])
        first_ss = sb("first_ss", [P, 3 * NT])
        first_rn = sb("first_rn", [P, 3 * NT])
        first_t = sb("first_t", [P, 3, 2 * NT])
        z = sb("z", [P, GT, D])
        q_ss = sb("q_ss", [P, 2, 4])
        q_t = sb("q_t", [P, 3, 4])
        q_rn = sb("q_rn", [P, 2, 4])
        z_sum = sb("z_sum", [P, 2, NT])
        rz = sb("rz", [P, 2, NT])
        z_copy = sb("z_copy", [P, GT, P])
        router_raw = sb("router_raw", [P, KC, E])
        router_sb = sb("router_sb", [P, 2, KC, E], F32R)
        logits = sb("logits", [P, GT, E])
        top = sb("top", [P, GT, 8])
        top_at = sb("top_at", [P, GT, 8], U32)
        top_f = sb("top_f", [P, GT, TOPK])
        r_d = sb("r_d", [P, GT])
        r_e = sb("r_e", [P, GT])
        r_den = sb("r_den", [P, GT])
        r_w = sb("r_w", [P, GT, TOPK])
        r_chosen = sb("r_chosen", [P, GT, TOPK, E])
        route = sb("route", [P, GT, 2 * E])

        early = ExitStack()
        wmod_sb = sb("wmod_sb", [P, KC, 6 * D], where=early)
        gate_sign = sb("gate_sign", [P, B, D], where=early)
        gout = sb("gout", [P, D], where=early)
        silu_rows = sb("silu_rows", [P, KC, B, P], where=early)
        z_second = sb("z_second", [P, GT, D], where=early)
        kn = sb("kn", [P, NT, DH], where=early)
        first_sq = sb("first_sq", [P, 3 * NT, DH], where=early)
        early.close()

        mid = ExitStack()
        psums = sb("psums", [P, 2, N], where=mid)
        oT = sb("oT", [P, 2, N], F32R, where=mid)
        wout_sb = sb("wout_sb", [P, 2, 2, D], F32R, where=mid)
        p32 = sb("p32", [P, 4, N], where=mid)
        phi = sb("phi", [P, 4, N], F32R, where=mid)
        plo = sb("plo", [P, 2, N], F32R, where=mid)
        kT1 = sb("kT1", [P, 2, N], F32R, where=mid)
        v1 = sb("v1", [P, 2, NT, DH], F32R, where=mid)
        qT = sb("qT", [P, 2, 2, N], F32R, where=mid)
        qn = sb("qn", [P, NT, 2, DH], where=mid)
        q_raw = sb("q_raw", [P, 2, 2, 2, DH], where=mid)
        q_sq = sb("q_sq", [P, 2, 2, DH], where=mid)
        wq_raw = sb("wq_raw", [P, KC, D], where=mid)
        wout_raw = sb("wout_raw", [P, 2, D], where=mid)
        wq_sb = sb("wq_sb", [P, 2, KC, D], F32R, where=mid)
        kT0 = sb("kT0", [P, 2, N], F32R, where=mid)
        v0 = sb("v0", [P, 2, NT, DH], F32R, where=mid)
        wkv_sb = sb("wkv_sb", [P, 2, KC, D], F32R, where=mid)
        wkv_raw = sb("wkv_raw", [P, KC, 2 * DH], where=mid)
        mid.close()
        kT, v = [kT0, kT1], [v0, v1]
        zs = [z, z_second]

        late = ExitStack()
        sb("still_used", [P, 2 * N + 2 * N + 2 * 2 * D], where=late)
        expert_w = sb("expert_w", [P, RT, 2, TILE], F32R, where=late)
        act_s = sb("act_s", [P, 2, BANK], where=late)
        act_u = sb("act_u", [P, BANK], where=late)
        act_a = sb("act_a", [P, 2, BANK], where=late)
        act_hi = sb("act_hi", [P, 2, BANK], F32R, where=late)
        act_lo = sb("act_lo", [P, 2, BANK], F32R, where=late)
        o_sb = sb("o_sb", [P, GT, D], where=late)
        loop_only = 10 * N + 2 * N + 2 * NT * DH + 4 * N + NT * 2 * DH + 8 * DH + 4 * DH + KC * D + 2 * D + 2 * KC * D
        sb("up_to_kT0", [P, loop_only - RT * 2 * TILE - 9 * BANK - GT * D - BANK], where=late)
        logits_T = sb("logits_T", [E, BANK], where=late)
        x_again = sb("x_again", [P, GT, D], where=late)
        rT = sb("rT", [2 * E, 2, BANK], F32R, where=late)
        rT_hi = sb("rT_hi", [2 * E, BANK], F32R, where=late)
        select = sb("select", [2 * E, ROWS], F32R, where=late)
        e_raw = sb("e_raw", [P, 2, TILE], where=late)
        late.close()

        pS = ctx.enter_context(nc.psum_tensor("pS", [P, 2, CH, BANK], F32))
        pO = ctx.enter_context(nc.psum_tensor("pO", [P, CH, BANK], F32))
        pX = ctx.enter_context(nc.psum_tensor("pX", [P, BANK], F32))
        pY = ctx.enter_context(nc.psum_tensor("pY", [P, BANK], F32))

        select_dram = nc.dram_tensor("select_dram", [2 * E, ROWS], F32, kind="Internal").ap()

        (dma_c, dma_const, dma_gout, dma_mod_first, dma_mod_rest, dma_wkv, dma_out, wq_in, wout_in,
         dma_router, dma_select, select_in) = map(sem, (
             "dma_c dma_const dma_gout dma_mod_first dma_mod_rest dma_wkv dma_out wq_in wout_in "
             "dma_router dma_select select_in").split())
        e_raw_in = [sem(f"e_raw_in{i}") for i in range(2)]
        dma_x = [sem(f"dma_x{g}") for g in range(GROUPS)]
        x_again_in = sem("x_again_in")
        (cond_exp, cond_den, silu_ready, mod_ready, mod_copied, mod_done) = map(sem, (
            "cond_exp cond_den silu_ready mod_ready mod_copied mod_done").split())
        constants_made = sem("constants_made")
        (ln_sem, stats_ready, rstd_chain, rstd_ready, normed, modulated) = map(sem, (
            "ln_sem stats_ready rstd_chain rstd_ready normed modulated").split())
        (wkv_hi_ready, wkv_lo_ready, wq_hi_ready, wq_lo_ready, wout_hi_ready, wout_lo_ready) = map(sem, (
            "wkv_hi_ready wkv_lo_ready wq_hi_ready wq_lo_ready wout_hi_ready wout_lo_ready").split())
        (x_job_ready, x_out) = map(sem, "x_job_ready x_out".split())
        (q_chain, q_rn_ready, qn_ready) = map(sem, "q_chain q_rn_ready qn_ready".split())
        (v_hi_ready, v_lo_ready) = map(sem, "v_hi_ready v_lo_ready".split())
        (scores_ready, phi_ready, p32_ready, plo_ready, psum_added, pv_done) = map(sem, (
            "scores_ready phi_ready p32_ready plo_ready psum_added pv_done").split())
        (o_hi_ready, o_lo_ready, y_job_ready, y_bank_free, rz_ready) = map(sem, (
            "o_hi_ready o_lo_ready y_job_ready y_bank_free rz_ready").split())
        (xt_ready, xt_hi_ready, xt_lo_ready) = map(sem, "xt_ready xt_hi_ready xt_lo_ready".split())
        (first_ready, first_squared, first_v_hi, first_v_lo, first_chain, first_scaled, first_t_ready,
         first_t_hi, first_t_lo) = map(sem, (
             "first_ready first_squared first_v_hi first_v_lo first_chain first_scaled first_t_ready "
             "first_t_hi first_t_lo").split())
        (top_ready, route_chain, exp_ready, route_ready) = map(sem, (
            "top_ready route_chain exp_ready route_ready").split())
        (router_hi, router_lo, gu_ready, cw_ready, silu_done, u_done, a_done, ahi_done, alo_done, down_done, o_mul,
         o_done, ehi_ready, elo_ready) = map(sem, (
             "router_hi router_lo gu_ready cw_ready silu_done u_done a_done ahi_done alo_done down_done o_mul "
             "o_done ehi_ready elo_ready").split())

        def next_q(it, b, jobs):
            return it + 1 if b or jobs is TURN else it

        def q_job(n, k):
            return 4 * n + k + 1

        def jobs_before(it, b):
            more = len(EARLY) - len(LOOP)
            early = more * min(it, 2) if isinstance(it, int) else more * 2
            return len(LOOP) * it + early + b * (len(TURN) - len(LOOP))

        def x_job(it, b, jobs, name):
            return jobs_before(it, b) + list(jobs).index(name) + 1

        def between_job(g, k):
            return jobs_before(ITERS - 1, B - 1) + len(END) + 5 * g + k + 1

        def y_job(head, k):
            return 6 * head + k + 1

        def added(it, s):
            it, s = it + s // STEPS, s % STEPS
            return 7 * (2 * it + s // NT) + max(s % NT, 1)

        def step(it, s):
            return STEPS * it + s

        def first_bank(i):
            return pS[:, i // 2, i % 2, :] if i < 4 else (pX[:, :], pY[:, :], pO[:, 0, :], pO[:, 1, :])[i - 4]

        def ln_first(g):
            return g if g < 2 else 2 * g

        def ln_second(g):
            return 2 + g if g < 2 else 2 * g + 1

        def ln_third(g):
            return 2 * GROUPS + 2 * g

        tokens = x.rearrange("b (t p) f -> p (b t) f", p=P)
        out_tokens = out.rearrange("b (t p) f -> p (b t) f", p=P)

        def iterations(eng, body):
            body(0, 0, True, EARLY)
            body(1, 0, False, EARLY)
            with eng.Fori(2, PAIRS - 1) as it:
                body(it, 0, False, LOOP)
            body(PAIRS - 1, 0, False, TURN)
            body(PAIRS, 1, True, LOOP)
            with eng.Fori(PAIRS + 1, ITERS - 1) as it:
                body(it, 1, False, LOOP)
            body(ITERS - 1, 1, False, END)

        block = ctx.enter_context(nc.Block())

        @block.sync
        def _(sp):
            def load_x(g):
                sp.dma_start(resid[:, GT * g:GT * g + GT, :], tokens[:, GT * g:GT * g + GT, :]).then_inc(dma_x[g], 16)

            def load_wq(pair):
                sp.dma_start(wq_raw[:, :, :].rearrange("p k f -> p (k f)"), wq[pair, :, :] if isinstance(pair, int) else
                             wq[bass.ds(pair, 1), :, :].rearrange("n p f -> p (n f)")).then_inc(wq_in, 16)

            def load_wout(pair):
                sp.dma_start(wout_raw[:, :, :].rearrange("p h f -> p (h f)"), wout[pair, :, :] if isinstance(pair, int) else
                             wout[bass.ds(pair, 1), :, :].rearrange("n p f -> p (n f)")).then_inc(wout_in, 16)

            wmod_view = wmod.rearrange("(k p) n -> p k n", p=P)
            sp.dma_start(condT[:, :, :], cond).then_inc(dma_c, 16)
            load_x(0)
            sp.dma_start(wmod_sb[:, :, 0:BANK], wmod_view[:, :, 0:BANK]).then_inc(dma_mod_first, 16)
            sp.dma_start(small[:, :], consts[:, 0:SMALL]).then_inc(dma_const, 16)
            sp.dma_start(gnorm[:, :], g_norm).then_inc(dma_const, 16)
            load_x(1)
            sp.dma_start(wmod_sb[:, :, BANK:6 * D], wmod_view[:, :, BANK:6 * D]).then_inc(dma_mod_rest, 16)
            sp.dma_start(wkv_raw[:, :, :], wkv.rearrange("(k p) n -> p k n", p=P)).then_inc(dma_wkv, 16)
            load_wq(0)
            load_wout(0)
            sp.dma_start(gout[:, :], g_out.rearrange("(a f) -> a f", a=1).broadcast_to([P, D])).then_inc(dma_gout, 16)
            load_x(2)
            load_x(3)
            sp.dma_start(router_raw[:, :, :], router.rearrange("(k p) e -> p k e", p=P)).then_inc(dma_router, 16)
            sp.dma_start(select_dram, consts[0:2 * E, SMALL:SMALL + ROWS]).then_inc(dma_select, 16)
            sp.wait_ge(wq_lo_ready, 1)
            load_wq(1)

            def loads(it, b):
                if not isinstance(it, int) or it + 2 < ITERS:
                    sp.wait_ge(wq_lo_ready, it + 2)
                    load_wq((it + 2) % PAIRS if isinstance(it, int) else it + 2 - PAIRS * b)
                if not isinstance(it, int) or it + 1 < ITERS:
                    sp.wait_ge(wout_lo_ready, it + 1)
                    load_wout((it + 1) % PAIRS if isinstance(it, int) else it + 1 - PAIRS * b)

            def load_x_again(g):
                if g:
                    sp.wait_ge(modulated, 2 * GROUPS + 4 * g - 2)
                sp.dma_start(x_again[:, :, :], tokens[:, GT * g:GT * g + GT, :]).then_inc(x_again_in, 16)

            def load_expert(t):
                sp.dma_start(e_raw[:, t % 2, :], experts_w[t, :, :]).then_inc(e_raw_in[t % 2], 16)

            with sp.Fori(0, PAIRS - 1) as it:
                loads(it, 0)
            loads(PAIRS - 1, 0)
            sp.wait_ge(pv_done, STEPS * PAIRS)
            load_x_again(0)
            with sp.Fori(PAIRS, ITERS - 2) as it:
                loads(it, 1)
            loads(ITERS - 2, 1)
            load_x_again(1)
            sp.wait_ge(dma_select, 16)
            sp.dma_start(select[:, :].bitcast(F32), select_dram).then_inc(select_in, 16)
            for t in range(2):
                load_expert(t)
            for t in range(2, RT):
                sp.wait_ge(elo_ready, t - 1)
                load_expert(t)
            for g in range(2, GROUPS):
                load_x_again(g)
            for g in range(GROUPS):
                sp.wait_ge(o_done, g + 1)
                sp.dma_start(out_tokens[:, GT * g:GT * g + GT, :], o_sb[:, :, :]).then_inc(dma_out, 16)
            sp.wait_ge(dma_out, 16 * GROUPS)

        @block.gpsimd
        def _(pool):
            minus_half, three_halves, eps_ln, eps_k, eps_q = (pool_c[:, i, :] for i in range(len(POOL_CONSTANTS)))
            for i, value in enumerate(POOL_CONSTANTS):
                nc.gpsimd.memset(pool_c[:, i, :], value).then_inc(constants_made, 1)
            nc.gpsimd.memset(ones[:, :], 1.0).then_inc(constants_made, 1)
            pool.wait_ge(constants_made, len(POOL_CONSTANTS) + 1)
            def newton(value, eps, t, dst, done, count):
                width = value.shape[-1]
                half, most, eps = minus_half[:, 0:width], three_halves[:, 0:width], eps[:, 0:width]
                steps = (
                    lambda: nc.gpsimd.tensor_tensor(t[0], value, eps, ALU.add),
                    lambda: nc.gpsimd.tensor_tensor(t[1], t[0], half, ALU.pow),
                    lambda: nc.gpsimd.tensor_tensor(t[2], t[1], t[1], ALU.mult),
                    lambda: nc.gpsimd.tensor_tensor(t[2], t[2], t[0], ALU.mult),
                    lambda: nc.gpsimd.tensor_tensor(t[2], t[2], half, ALU.mult),
                    lambda: nc.gpsimd.tensor_tensor(t[2], t[2], most, ALU.add),
                )
                for i, make in enumerate(steps):
                    make().then_inc(done, 1)
                    pool.wait_ge(done, count + i + 1)
                return nc.gpsimd.tensor_tensor(dst, t[1], t[2], ALU.mult)

            def rstd(n):
                pool.wait_ge(stats_ready, n + 1)
                t = [ln_t[:, i, :] for i in range(3)]
                newton(ln_mv[:, n, :, 1], eps_ln, t, ln_r[:, n, :], rstd_chain, 8 * n).then_inc(rstd_chain, 1)
                pool.wait_ge(rstd_chain, 8 * n + 7)
                nc.gpsimd.tensor_tensor(t[0], ln_mv[:, n, :, 0], ln_r[:, n, :], ALU.mult).then_inc(rstd_chain, 1)
                pool.wait_ge(rstd_chain, 8 * n + 8)
                nc.gpsimd.tensor_scalar(ln_nb[:, n, :], t[0], -1.0, None, ALU.mult).then_inc(rstd_ready, 1)
                pool.wait_ge(rstd_ready, n + 1)

            def q_norm(n, k, eps, job):
                pool.wait_ge(x_out, 2 * job)
                if not (isinstance(n, int) and n == 0 and k < 2):
                    pool.wait_ge(qn_ready, q_job(n, k) - 2)
                newton(q_ss[:, k % 2, :], eps, [q_t[:, i, :] for i in range(3)], q_rn[:, k % 2, :],
                       q_chain, 6 * (q_job(n, k) - 1)).then_inc(q_rn_ready, 1)
                pool.wait_ge(q_rn_ready, q_job(n, k))

            for n in range(4):
                rstd(n)
            for i, (eps, lo, hi, jobs) in enumerate(((eps_k, 0, NT, 4), (eps_q, NT, 3 * NT, 8))):
                pool.wait_ge(first_squared, jobs)
                newton(first_ss[:, lo:hi], eps, [first_t[:, j, 0:hi - lo] for j in range(3)], first_rn[:, lo:hi],
                       first_chain, 7 * i).then_inc(first_chain, 1)
                pool.wait_ge(first_chain, 7 * i + 7)

            def norms(it, b, first, jobs):
                if jobs is EARLY:
                    rstd(ln_first(2 + it))
                for name in jobs:
                    k = int(name[-1])
                    if name[:-1] == "KV":
                        q_norm(PAIRS - 1, k, eps_k, x_job(it, b, jobs, name))
                    if name[:-1] == "Q":
                        q_norm(next_q(it, b, jobs), k, eps_q, x_job(it, b, jobs, name))
                    if jobs is EARLY and name == "Q1":
                        rstd(ln_second(2 + it))
                    if first and b and name == "Q2":
                        rstd(ln_third(0))
                if first and b:
                    rstd(ln_third(0) + 1)

            iterations(pool, norms)
            for g in range(1, GROUPS):
                for n in (ln_third(g), ln_third(g) + 1):
                    rstd(n)

        @block.scalar
        def _(act):
            act.wait_ge(dma_c, 16)
            nc.scalar.activation(cond_e[:, :, :], condT[:, :, :], ACT.Exp, scale=-1.0).then_inc(cond_exp, 1)
            def mod_rows(c):
                for b in range(B):
                    act.wait_ge(mod_ready, B * c + b + 1)
                    src = (pO[:, b, :], pS[:, 1, b, :], pS[:, 0, b, :])[c].rearrange("p (a f) -> p a f", a=2)
                    nc.scalar.copy(mod[:, b, 2 * c:2 * c + 2, :], src).then_inc(mod_copied, 1)

            def normalise(n, src, dst=z):
                act.wait_ge(rstd_ready, n + 1)
                for t in range(GT):
                    nc.scalar.activation(dst[:, t, :], src[:, t, :], ACT.Identity, scale=ln_r[:, n, t:t + 1],
                                         bias=ln_nb[:, n, t:t + 1]).then_inc(normed, 1)

            def split_wq_hi(pair):
                act.wait_ge(wq_in, 16 * (pair + 1))
                for k in range(KC):
                    ins = nc.scalar.activation(wq_sb[:, HI, k, :], wq_raw[:, k, :], ACT.Copy, scale=gnorm[:, k:k + 1])
                ins.then_inc(wq_hi_ready, 1)

            def split_wout_hi(pair, used):
                act.wait_ge(wout_in, 16 * (pair + 1))
                if used is not None:
                    act.wait_ge(y_job_ready, used)
                nc.scalar.copy(wout_sb[:, :, HI, :], wout_raw[:, :, :]).then_inc(wout_hi_ready, 1)

            def chunk(c):
                return slice(c * BANK, (c + 1) * BANK)

            mod_rows(0)
            for g in range(2):
                normalise(ln_first(g), resid[:, GT * g:GT * g + GT, :], zs[g])
            act.wait_ge(dma_const, 16 * 2)
            act.wait_ge(dma_wkv, 16)
            for k in range(KC):
                nc.scalar.activation(wkv_sb[:, HI, k, :], wkv_raw[:, k, :], ACT.Copy, scale=gnorm[:, k:k + 1]).then_inc(wkv_hi_ready, 1)
            split_wq_hi(0)
            mod_rows(1)
            mod_rows(2)
            for g in range(2):
                act.wait_ge(modulated, 2 * g + 2)
                normalise(ln_second(g), zs[g], zs[g])
            for g in range(2):
                for k in range(KC):
                    act.wait_ge(xt_ready, KC * g + k + 1)
                    nc.scalar.copy(xT[0][:, HI, k, chunk(g)], first_bank(4 + 2 * g + k)).then_inc(xt_hi_ready, 1)

            for i in range(8):
                act.wait_ge(first_ready, i + 1)
                src = first_bank(i).rearrange("p (t h d) -> p t h d", t=2, h=2)
                blocks = [(t, 0, 2 * i + t) for t in range(2)] if i < 4 else \
                         [(t, h, NT + 4 * (i - 4) + 2 * t + h) for t in range(2) for h in range(2)]
                if i < 4:
                    nc.scalar.copy(v[0][:, HI, 2 * i:2 * i + 2, :], src[:, :, 1, :]).then_inc(first_v_hi, 1)
                for t, h, at in blocks:
                    ins = nc.scalar.activation(first_sq[:, at, :], src[:, t, h, :], ACT.Square, accum_out=first_ss[:, at:at + 1])
                ins.then_inc(first_squared, 1)

            def q_copy(n, k, job, values=None, after_kv=False):
                act.wait_ge(x_job_ready, job)
                if not (isinstance(n, int) and n == 0 and k < 2):
                    act.wait_ge(qn_ready, q_job(n, k) - 2)
                if values is not None and k >= 2:
                    act.wait_ge(v_lo_ready, k - 1)
                if after_kv and k < 2:
                    act.wait_ge(v_lo_ready, 3 + k)
                src = pX[:, :].rearrange("p (t h d) -> p (t h) d", t=2, h=2)
                nc.scalar.copy(q_raw[:, k % 2, :, :, :].rearrange("p t h d -> p (t h) d"), src).then_inc(x_out, 1)
                for i in range(4):
                    ins = nc.scalar.activation(q_sq[:, i // 2, i % 2, :], src[:, i, :], ACT.Square, accum_out=q_ss[:, k % 2, i:i + 1])
                ins.then_inc(x_out, 1)
                if values is not None:
                    act.wait_ge(x_out, 2 * job)
                    nc.scalar.copy(v[values][:, HI, 2 * k:2 * k + 2, :], q_raw[:, k % 2, :, 1, :]).then_inc(v_hi_ready, 1)

            def t_hi(dst, job):
                act.wait_ge(x_job_ready, job)
                nc.scalar.copy(dst, pX[:, :]).then_inc(x_out, 1)

            for i in range(4):
                act.wait_ge(first_t_ready, i + 1)
                dst = kT[0] if i < 2 else qT[:, 0]
                nc.scalar.copy(dst[:, HI, chunk(i % 2)], first_bank(i)).then_inc(first_t_hi, 1)
            act.wait_ge(dma_router, 16)
            nc.scalar.copy(router_sb[:, HI, :, :], router_raw[:, :, :]).then_inc(router_hi, 1)

            def o_hi(head, free):
                act.wait_ge(pv_done, NT * (head + 1))
                if free:
                    act.wait_ge(y_job_ready, y_job(head - 1, 5))
                for c in range(CH):
                    nc.scalar.copy(oT[:, HI, chunk(c)], pO[:, c, :]).then_inc(o_hi_ready, 1)

            def between_norms(slot):
                for g in range(GROUPS):
                    stage = stage_of(g, slot)
                    if stage == "normalise_1":
                        if g:
                            act.wait_ge(x_job_ready, between_job(g - 1, 1))
                        normalise(ln_third(g), resid[:, GT * g:GT * g + GT, :])
                    if stage == "normalise_2":
                        normalise(ln_third(g) + 1, resid[:, GT * g:GT * g + GT, :])
                    if stage_of(g, slot - 1) == "top_two":
                        act.wait_ge(top_ready, g + 1)
                        nc.scalar.activation(r_e[:, :], r_d[:, :], ACT.Exp).then_inc(exp_ready, 1)

            def between_bank(slot):
                for g in range(GROUPS):
                    stage = stage_of(g, slot)
                    if stage in TRANSPOSES:
                        k, c = TRANSPOSES.index(stage), g % 2
                        t_hi(xT[g // 2][:, HI, k, chunk(c)], between_job(g, k))
                    if stage == "route_t":
                        act.wait_ge(x_job_ready, between_job(g, 4))
                        if g:
                            act.wait_ge(x_out, 2 * between_job(g - 1, 4))
                        nc.scalar.copy(rT_hi[:, :], pX[0:2 * E, :]).then_inc(x_out, 1)

            def split_hi(t):
                act.wait_ge(e_raw_in[t % 2], 16 * (t // 2 + 1))
                nc.scalar.copy(expert_w[:, t, HI, :], e_raw[:, t % 2, :]).then_inc(ehi_ready, 1)

            def entry(slot, g):
                if slot == ENTRY["normalise_1"]:
                    if g == GROUPS - 1:
                        act.wait_ge(x_job_ready, x_job(g - 3, 0, EARLY, "N1"))
                    normalise(ln_first(g), resid[:, GT * g:GT * g + GT, :])
                if slot == ENTRY["normalise_2"]:
                    act.wait_ge(modulated, 2 * g + 2)
                    normalise(ln_second(g), z)

            def bank_x(it, b, jobs, name):
                k, job = int(name[-1]), x_job(it, b, jobs, name)
                if name[:-1] == "B":
                    t_hi(qT[:, 1, HI, chunk(k)], job)
                if name[:-1] == "A":
                    t_hi(qT[:, 0, HI, chunk(k)], job)
                if name[:-1] == "KT":
                    t_hi(kT[1][:, HI, chunk(k)], job)
                if name[:-1] == "N":
                    t_hi(xT[1][:, HI, k, chunk(it)], job)
                if name[:-1] == "KV":
                    q_copy(PAIRS - 1, k, job, values=1)
                if name[:-1] == "Q":
                    q_copy(next_q(it, b, jobs), k, job, after_kv=jobs is TURN)

            def row_sums(head, parity, c):
                act.wait_ge(y_job_ready, y_job(head, c))
                for t in range(GT):
                    ins = nc.scalar.activation(z_copy[:, t, :], pY[:, t * P:(t + 1) * P], ACT.Copy, accum_out=z_sum[:, parity, GT * c + t:GT * c + t + 1])
                ins.then_inc(y_bank_free, 1)

            def steps(it, b, first, jobs):
                start, end = b == 0 and first, jobs is END
                for s in range(STEPS):
                    t = step(it, s)
                    act.wait_ge(scores_ready, t + 1)
                    if not (start and s < 4):
                        act.wait_ge(pv_done, t - 3)
                    nc.scalar.activation(phi[:, s % 4, :].rearrange("p (c n) -> p c n", c=CH), pS[:, s % 2, :, :],
                                         ACT.Exp, scale=16.0).then_inc(phi_ready, 1)
                    if not (start and s < 4):
                        act.wait_ge(psum_added, added(it, s - 4))
                    nc.scalar.activation(p32[:, s % 4, :].rearrange("p (c n) -> p c n", c=CH), pS[:, s % 2, :, :],
                                         ACT.Exp, scale=16.0).then_inc(p32_ready, 1)
                    if s == 0 and not start:
                        o_hi(2 * it - 1, True)
                    if s == NT:
                        o_hi(2 * it, not start)
                    for name in jobs:
                        if jobs[name] == s:
                            bank_x(it, b, jobs, name)
                    if s in ZB_AT and not start:
                        row_sums(2 * it - 1, 1, ZB_AT.index(s))
                    if s in ZA_AT:
                        row_sums(2 * it, 0, ZA_AT.index(s))
                    if s == WQ_SPLIT and not end:
                        split_wq_hi(it + 1)
                    if s == WOUT_SPLIT:
                        split_wout_hi(it, None if start else y_job(2 * it - 1, 5))
                    if jobs is EARLY:
                        entry(s, 2 + it)
                    if first and b or end:
                        between_bank(s if end else s - STEPS)
                        between_norms(s if end else s - STEPS)

            iterations(act, steps)
            o_hi(2 * ITERS - 1, True)

            for c in range(CH):
                row_sums(2 * ITERS - 1, 1, c)
            act.wait_ge(psum_added, 7 * 2 * ITERS)
            for t in range(AHEAD):
                split_hi(t)
            for n in range(GROUPS * RT):
                act.wait_ge(gu_ready, n + 1)
                if n >= 2:
                    act.wait_ge(u_done, n - 1)
                nc.scalar.activation(act_s[:, n % 2, :], pS[:, n % 2, 0, :], ACT.Silu).then_inc(silu_done, 1)
                between_bank(STEPS + n)
                act.wait_ge(a_done, n + 1)
                if n >= 2:
                    act.wait_ge(down_done, n - 1)
                nc.scalar.copy(act_hi[:, n % 2, :], act_a[:, n % 2, :]).then_inc(ahi_done, 1)
                if n + AHEAD < RT:
                    split_hi(n + AHEAD)
                between_norms(STEPS + n)

        @block.vector
        def _(dve):
            dve.wait_ge(cond_exp, 1)
            nc.vector.tensor_scalar(cond_e[:, :, :], cond_e[:, :, :], 1.0, None, ALU.add).then_inc(cond_den, 1)
            dve.wait_ge(cond_den, 1)
            nc.vector.reciprocal(cond_e[:, :, :], cond_e[:, :, :]).then_inc(cond_den, 1)
            dve.wait_ge(cond_den, 2)
            nc.vector.tensor_tensor(condT[:, :, :], condT[:, :, :], cond_e[:, :, :], ALU.mult).then_inc(cond_den, 1)
            dve.wait_ge(cond_den, 3)
            nc.vector.tensor_copy(silu_rows[:, :, :, :], condT[:, :, :].unsqueeze(3).broadcast_to([P, KC, B, P])).then_inc(silu_ready, 1)

            def ln(n, src, count=None):
                for t in range(GT):
                    ins = nc.vector.bn_stats(ln_stats[:, n, t, :], src[:, t, :])
                ins.then_inc(ln_sem, 1)
                dve.wait_ge(ln_sem, n + 1)
                for t in range(GT):
                    ins = nc.vector.bn_aggr(ln_mv[:, n, t, :], ln_stats[:, n, t, :])
                ins.then_inc(stats_ready, 1)

            def rows(b, which):
                return mod[:, b, which, :].unsqueeze(1).broadcast_to([P, GT, D])

            def modulate(b, half_rows, count, normed_count, z=z):
                dve.wait_ge(normed, normed_count)
                nc.vector.tensor_tensor(z[:, :, :], z[:, :, :], rows(b, half_rows + SCALE), ALU.mult).then_inc(modulated, 1)
                dve.wait_ge(modulated, count)
                nc.vector.tensor_tensor(z[:, :, :], z[:, :, :], rows(b, half_rows + SHIFT), ALU.add).then_inc(modulated, 1)
                dve.wait_ge(modulated, count + 1)

            def chunk(c):
                return slice(c * BANK, (c + 1) * BANK)

            def split_wq_lo(pair):
                dve.wait_ge(wq_hi_ready, pair + 1)
                for k in range(KC):
                    ins = nc.vector.scalar_tensor_tensor(out=wq_sb[:, LO, k, :], in0=wq_raw[:, k, :], scalar=gnorm[:, k:k + 1],
                                                         in1=wq_sb[:, HI, k, :], op0=ALU.mult, op1=ALU.subtract)
                ins.then_inc(wq_lo_ready, 1)

            def split_wout_lo(pair):
                dve.wait_ge(wout_hi_ready, pair + 1)
                nc.vector.tensor_tensor(wout_sb[:, :, LO, :], wout_raw[:, :, :], wout_sb[:, :, HI, :], ALU.subtract).then_inc(wout_lo_ready, 1)

            def gate_rows(i):
                h, done = 3 * i + GATE, 2 + 4 * i
                nc.vector.tensor_scalar(gate_sign[:, :, :], mod[:, :, h, :], 0.0, 2.0, ALU.is_ge, ALU.mult).then_inc(mod_done, 1)
                nc.vector.scalar_tensor_tensor(out=mod[:, :, h, :], in0=mod[:, :, h, :], scalar=-1.0, in1=mod[:, :, h, :],
                                               op0=ALU.mult, op1=ALU.max).then_inc(mod_done, 1)
                dve.wait_ge(mod_done, done + 2)
                nc.vector.tensor_scalar(mod[:, :, h, :], mod[:, :, h, :], 0.25, None, ALU.max).then_inc(mod_done, 1)
                dve.wait_ge(mod_done, done + 3)
                nc.vector.scalar_tensor_tensor(out=mod[:, :, h, :], in0=gate_sign[:, :, :], scalar=-1.0, in1=mod[:, :, h, :],
                                               op0=ALU.add, op1=ALU.mult).then_inc(mod_done, 1)
                dve.wait_ge(mod_done, done + 4)

            for g in range(2):
                dve.wait_ge(dma_x[g], 16)
                ln(ln_first(g), resid[:, GT * g:GT * g + GT, :])
            dve.wait_ge(mod_copied, 2)
            nc.vector.tensor_scalar(mod[:, :, SCALE, :], mod[:, :, SCALE, :], 1.0, None, ALU.add).then_inc(mod_done, 1)
            dve.wait_ge(mod_done, 1)
            for g in range(2):
                modulate(0, 0, 2 * g + 1, GT * (ln_first(g) + 1), zs[g])
                ln(ln_second(g), zs[g])
            for k in range(KC):
                dve.wait_ge(wkv_hi_ready, k + 1)
                nc.vector.scalar_tensor_tensor(out=wkv_sb[:, LO, k, :], in0=wkv_raw[:, k, :], scalar=gnorm[:, k:k + 1],
                                               in1=wkv_sb[:, HI, k, :], op0=ALU.mult, op1=ALU.subtract).then_inc(wkv_lo_ready, 1)
            split_wq_lo(0)
            for g in range(2):
                for k in range(KC):
                    dve.wait_ge(xt_hi_ready, KC * g + k + 1)
                    nc.vector.tensor_tensor(xT[0][:, LO, k, chunk(g)], first_bank(4 + 2 * g + k), xT[0][:, HI, k, chunk(g)], ALU.subtract).then_inc(xt_lo_ready, 1)

            def q_apply(n, k):
                dve.wait_ge(q_rn_ready, q_job(n, k))
                nc.vector.tensor_tensor(qn[:, 2 * k:2 * k + 2, :, :].rearrange("p t h d -> p (t h) d"),
                                        q_raw[:, k % 2, :, :, :].rearrange("p t h d -> p (t h) d"),
                                        q_rn[:, k % 2, :].unsqueeze(2).broadcast_to([P, 4, DH]), ALU.mult).then_inc(qn_ready, 1)

            def v_lo(b, k):
                dve.wait_ge(v_hi_ready, k + 1)
                nc.vector.tensor_tensor(v[b][:, LO, 2 * k:2 * k + 2, :], q_raw[:, k % 2, :, 1, :],
                                        v[b][:, HI, 2 * k:2 * k + 2, :], ALU.subtract).then_inc(v_lo_ready, 1)

            def t_lo(hi, dst, job):
                dve.wait_ge(x_out, 2 * job - 1)
                nc.vector.tensor_tensor(dst, pX[:, :], hi, ALU.subtract).then_inc(x_out, 1)

            for i in range(4):
                dve.wait_ge(first_v_hi, i + 1)
                dve.wait_ge(first_squared, i + 1)
                nc.vector.tensor_tensor(v[0][:, LO, 2 * i:2 * i + 2, :], first_bank(i).rearrange("p (t h d) -> p t h d", t=2, h=2)[:, :, 1, :],
                                        v[0][:, HI, 2 * i:2 * i + 2, :], ALU.subtract).then_inc(first_v_lo, 1)
            dve.wait_ge(first_chain, 7)
            for i in range(4):
                nc.vector.tensor_tensor(kn[:, 2 * i:2 * i + 2, :], first_bank(i).rearrange("p (t h d) -> p t h d", t=2, h=2)[:, :, 0, :],
                                        first_rn[:, 2 * i:2 * i + 2].unsqueeze(2).broadcast_to([P, 2, DH]), ALU.mult).then_inc(first_scaled, 1)

            def first_lo(i):
                dve.wait_ge(first_t_hi, i + 1)
                dst = kT[0] if i < 2 else qT[:, 0]
                nc.vector.tensor_tensor(dst[:, LO, chunk(i % 2)], first_bank(i), dst[:, HI, chunk(i % 2)], ALU.subtract).then_inc(first_t_lo, 1)

            dve.wait_ge(mod_copied, 6)
            nc.vector.tensor_scalar(mod[:, :, 3 + SCALE, :], mod[:, :, 3 + SCALE, :], 1.0, None, ALU.add).then_inc(mod_done, 1)
            dve.wait_ge(mod_done, 2)
            for i in range(2):
                first_lo(i)
            gate_rows(0)
            dve.wait_ge(first_chain, 14)
            for i in range(4):
                nc.vector.tensor_tensor(qn[:, 2 * i:2 * i + 2, :, :].rearrange("p t h d -> p (t h) d"),
                                        first_bank(4 + i).rearrange("p (b d) -> p b d", d=DH),
                                        first_rn[:, NT + 4 * i:NT + 4 * i + 4].unsqueeze(2).broadcast_to([P, 4, DH]), ALU.mult).then_inc(first_scaled, 1)
            for i in range(2, 4):
                first_lo(i)
            gate_rows(1)
            dve.wait_ge(dma_gout, 16)
            nc.vector.tensor_tensor(mod[:, :, GATE, :], mod[:, :, GATE, :], gout[:, :].unsqueeze(1).broadcast_to([P, B, D]), ALU.mult).then_inc(mod_done, 1)
            dve.wait_ge(router_hi, 1)
            nc.vector.tensor_tensor(router_sb[:, LO, :, :], router_raw[:, :, :], router_sb[:, HI, :, :], ALU.subtract).then_inc(router_lo, 1)

            def o_lo(head):
                for c in range(CH):
                    dve.wait_ge(o_hi_ready, CH * head + c + 1)
                    nc.vector.tensor_tensor(oT[:, LO, chunk(c)], pO[:, c, :], oT[:, HI, chunk(c)], ALU.subtract).then_inc(o_lo_ready, 1)

            def row_sums(head, parity):
                dve.wait_ge(y_bank_free, y_job(head, 1))
                nc.vector.reciprocal(rz[:, parity, :], z_sum[:, parity, :]).then_inc(rz_ready, 1)

            def add_head(head, k, parity, b, new):
                dve.wait_ge(y_job_ready, y_job(head, k + 2))
                dve.wait_ge(rz_ready, head + 1)
                for i in range(2):
                    t = 2 * k + i
                    dst = resid[:, NT * b + t, :]
                    src = pY[:, i * D:(i + 1) * D]
                    if new:
                        ins = nc.vector.tensor_scalar(dst, src, rz[:, parity, t:t + 1], None, ALU.mult)
                    else:
                        ins = nc.vector.scalar_tensor_tensor(out=dst, in0=src, scalar=rz[:, parity, t:t + 1], in1=dst,
                                                             op0=ALU.mult, op1=ALU.add)
                ins.then_inc(y_bank_free, 1)

            chain = [0]

            def link(ins):
                chain[0] += 1
                ins.then_inc(route_chain, 1)
                dve.wait_ge(route_chain, chain[0])

            def between(slot):
                for g in range(GROUPS):
                    stage = stage_of(g, slot)
                    b, m = g // 2, 2 * GROUPS + 4 * g
                    here = resid[:, GT * g:GT * g + GT, :]
                    if stage == "stats_1":
                        dve.wait_ge(y_bank_free, y_job(HEADS * (b + 1) - 1, 5))
                        ln(ln_third(g), here)
                    if stage == "gate_multiply":
                        dve.wait_ge(normed, 2 * GT * GROUPS + 2 * GT * g + GT)
                        nc.vector.tensor_tensor(z[:, :, :], z[:, :, :], rows(b, GATE), ALU.mult).then_inc(modulated, 1)
                    if stage == "gate_add":
                        dve.wait_ge(modulated, m + 1)
                        dve.wait_ge(x_again_in, 16 * (g + 1))
                        nc.vector.tensor_tensor(here, z[:, :, :], x_again[:, :, :], ALU.add).then_inc(modulated, 1)
                    if stage == "stats_2":
                        dve.wait_ge(modulated, m + 2)
                        ln(ln_third(g) + 1, here)
                    if stage == "modulate_scale":
                        dve.wait_ge(normed, 2 * GT * GROUPS + 2 * GT * g + 2 * GT)
                        nc.vector.tensor_tensor(z[:, :, :], z[:, :, :], rows(b, 3 + SCALE), ALU.mult).then_inc(modulated, 1)
                    if stage == "modulate_shift":
                        dve.wait_ge(modulated, m + 3)
                        nc.vector.tensor_tensor(z[:, :, :], z[:, :, :], rows(b, 3 + SHIFT), ALU.add).then_inc(modulated, 1)
                    if stage in TRANSPOSES:
                        k, c = TRANSPOSES.index(stage), g % 2
                        t_lo(xT[b][:, HI, k, chunk(c)], xT[b][:, LO, k, chunk(c)], between_job(g, k))
                    if stage == "logits":
                        dve.wait_ge(x_job_ready, between_job(g, 2))
                        nc.vector.tensor_copy(logits_T[:, :], pX[0:E, :]).then_inc(x_out, 2)
                    if stage == "top_two":
                        dve.wait_ge(x_job_ready, between_job(g, 3))
                        nc.vector.tensor_copy(logits[:, :, :], pX[:, 0:GT * E].rearrange("p (t e) -> p t e", e=E)).then_inc(x_out, 2)
                        dve.wait_ge(x_out, 2 * between_job(g, 3))
                        for t in range(GT):
                            ins = nc.vector.max(top[:, t, :], logits[:, t, :])
                        link(ins)
                        for t in range(GT):
                            ins = nc.vector.max_index(top_at[:, t, :], top[:, t, :], logits[:, t, :])
                        link(ins)
                        link(nc.vector.tensor_copy(top_f[:, :, :], top_at[:, :, 0:TOPK]))
                        nc.vector.tensor_tensor(r_d[:, :], top[:, :, 1], top[:, :, 0], ALU.subtract).then_inc(top_ready, 1)
                        link(nc.vector.tensor_tensor(r_chosen[:, :, :, :], experts.unsqueeze(1).unsqueeze(1).broadcast_to([P, GT, TOPK, E]),
                                                     top_f[:, :, :].unsqueeze(3).broadcast_to([P, GT, TOPK, E]), ALU.is_equal))
                    if stage == "weights":
                        dve.wait_ge(exp_ready, g + 1)
                        link(nc.vector.tensor_scalar(r_den[:, :], r_e[:, :], 1.0, None, ALU.add))
                        link(nc.vector.reciprocal(r_w[:, :, 0], r_den[:, :]))
                        link(nc.vector.tensor_tensor(r_w[:, :, 1], r_w[:, :, 0], r_e[:, :], ALU.mult))
                        link(nc.vector.tensor_tensor(r_chosen[:, :, :, :], r_chosen[:, :, :, :],
                                                     r_w[:, :, :].unsqueeze(3).broadcast_to([P, GT, TOPK, E]), ALU.mult))
                        if g:
                            dve.wait_ge(x_job_ready, between_job(g - 1, 4))
                        nc.vector.tensor_tensor(route[:, :, 0:E], r_chosen[:, :, 0, :], r_chosen[:, :, 1, :], ALU.add)
                        nc.vector.tensor_tensor(route[:, :, E:2 * E], r_chosen[:, :, 0, :], r_chosen[:, :, 1, :], ALU.add).then_inc(route_ready, 1)
                    if stage == "route_t":
                        dve.wait_ge(x_out, 2 * between_job(g, 4) - 1)
                        if g >= 2:
                            dve.wait_ge(cw_ready, RT * (g - 1))
                        nc.vector.scalar_tensor_tensor(out=rT[:, g % 2, :], in0=rT_hi[:, :], scalar=small[0:2 * E, P:P + 1],
                                                       in1=pX[0:2 * E, :], op0=ALU.mult, op1=ALU.add).then_inc(x_out, 1)

            def split_lo(t):
                dve.wait_ge(ehi_ready, t + 1)
                nc.vector.tensor_tensor(expert_w[:, t, LO, :], e_raw[:, t % 2, :], expert_w[:, t, HI, :], ALU.subtract).then_inc(elo_ready, 1)

            def entry(slot, g):
                if slot == ENTRY["stats_1"]:
                    dve.wait_ge(dma_x[g], 16)
                    ln(ln_first(g), resid[:, GT * g:GT * g + GT, :])
                if slot == ENTRY["modulate_scale"]:
                    dve.wait_ge(normed, GT * (ln_first(g) + 1))
                    nc.vector.tensor_tensor(z[:, :, :], z[:, :, :], rows(1, SCALE), ALU.mult).then_inc(modulated, 1)
                if slot == ENTRY["modulate_shift"]:
                    dve.wait_ge(modulated, 2 * g + 1)
                    nc.vector.tensor_tensor(z[:, :, :], z[:, :, :], rows(1, SHIFT), ALU.add).then_inc(modulated, 1)
                if slot == ENTRY["stats_2"]:
                    dve.wait_ge(modulated, 2 * g + 2)
                    ln(ln_second(g), z)

            def bank_x(it, b, jobs, name):
                k, job = int(name[-1]), x_job(it, b, jobs, name)
                if name[:-1] == "B":
                    t_lo(qT[:, 1, HI, chunk(k)], qT[:, 1, LO, chunk(k)], job)
                if name[:-1] == "A":
                    t_lo(qT[:, 0, HI, chunk(k)], qT[:, 0, LO, chunk(k)], job)
                if name[:-1] == "KT":
                    t_lo(kT[1][:, HI, chunk(k)], kT[1][:, LO, chunk(k)], job)
                if name[:-1] == "N":
                    t_lo(xT[1][:, HI, k, chunk(it)], xT[1][:, LO, k, chunk(it)], job)
                if name[:-1] == "KV":
                    v_lo(1, k)

            def steps(it, b, first, jobs):
                start, end = b == 0 and first, jobs is END
                before_b = b - 1 if first else b
                for s in range(STEPS):
                    t, head, j = step(it, s), 2 * it + s // NT, s % NT
                    dve.wait_ge(p32_ready, t + 1)
                    if not (start and s < 2):
                        dve.wait_ge(pv_done, t - 1)
                    nc.vector.tensor_tensor(plo[:, s % 2, :], p32[:, s % 4, :], phi[:, s % 4, :], ALU.subtract).then_inc(plo_ready, 1)
                    if s == 0 and not start:
                        o_lo(2 * it - 1)
                    if s == NT:
                        o_lo(2 * it)
                    for name in jobs:
                        if jobs[name] == s:
                            bank_x(it, b, jobs, name)
                    if not start:
                        if s == OB_AT[0]:
                            row_sums(2 * it - 1, 1)
                        if s in OB_AT:
                            add_head(2 * it - 1, OB_AT.index(s), 1, before_b, False)
                    if s == OA_AT[0]:
                        row_sums(2 * it, 0)
                    if s in OA_AT:
                        add_head(2 * it, OA_AT.index(s), 0, b, first)
                    if s == WQ_SPLIT and not end:
                        split_wq_lo(it + 1)
                    for name, at in APPLY[len(jobs)].items():
                        if at == s:
                            k = int(name[-1])
                            q_apply(PAIRS - 1 if name[:-1] == "KV" else next_q(it, b, jobs), k)
                    if j:
                        total = psums[:, (s // NT) % 2, :]
                        if j == 1 and not start:
                            dve.wait_ge(y_job_ready, y_job(head - 2, 1))
                        if j > 1:
                            dve.wait_ge(psum_added, 7 * head + j - 1)
                        nc.vector.tensor_tensor(total, p32[:, (s - 1) % 4, :] if j == 1 else total, p32[:, s % 4, :], ALU.add).then_inc(psum_added, 1)
                    if s == WOUT_SPLIT:
                        split_wout_lo(it)
                    if jobs is EARLY:
                        entry(s, 2 + it)
                    if first and b or end:
                        between(s if end else s - STEPS)

            iterations(dve, steps)
            o_lo(2 * ITERS - 1)
            split_lo(0)
            row_sums(2 * ITERS - 1, 1)
            for k in range(4):
                add_head(2 * ITERS - 1, k, 1, B - 1, False)
                if k == 1:
                    split_lo(1)
            for t in range(2, AHEAD):
                split_lo(t)

            def output_gate(g):
                dve.wait_ge(down_done, RT * (g + 1))
                if g:
                    dve.wait_ge(dma_out, 16 * g)
                nc.vector.tensor_tensor(o_sb[:, :, :], pO[:, :, :].rearrange("p c (t f) -> p (c t) f", f=D), rows(g // 2, 3 + GATE), ALU.mult).then_inc(o_mul, 1)

            def output_add(g):
                dve.wait_ge(o_mul, g + 1)
                nc.vector.tensor_tensor(o_sb[:, :, :], o_sb[:, :, :], resid[:, GT * g:GT * g + GT, :], ALU.add).then_inc(o_done, 1)

            for n in range(GROUPS * RT):
                dve.wait_ge(silu_done, n + 1)
                if n:
                    dve.wait_ge(a_done, n)
                nc.vector.tensor_tensor(act_u[:, :], act_s[:, n % 2, :], pS[:, n % 2, 1, :], ALU.mult).then_inc(u_done, 1)
                dve.wait_ge(u_done, n + 1)
                dve.wait_ge(cw_ready, n + 1)
                if n >= 2:
                    dve.wait_ge(ahi_done, n - 1)
                nc.vector.tensor_tensor(act_a[:, n % 2, :], act_u[:, :], pY[:, :], ALU.mult).then_inc(a_done, 1)
                if n and n % RT == 0:
                    output_gate(n // RT - 1)
                between(STEPS + n)
                dve.wait_ge(ahi_done, n + 1)
                nc.vector.tensor_tensor(act_lo[:, n % 2, :], act_a[:, n % 2, :], act_hi[:, n % 2, :], ALU.subtract).then_inc(alo_done, 1)
                if n + AHEAD < RT:
                    split_lo(n + AHEAD)
                if n >= RT and n % RT == 3:
                    output_add(n // RT - 1)
            output_gate(GROUPS - 1)
            output_add(GROUPS - 1)

        @block.tensor
        def _(pe):
            def mod_rows(c):
                for b in range(B):
                    dst = (pO[:, b, :], pS[:, 1, b, :], pS[:, 0, b, :])[c]
                    for k in range(KC):
                        mm = pe.matmul(dst, silu_rows[:, k, b, :], wmod_sb[:, k, c * BANK:(c + 1) * BANK], start=(k == 0), stop=(k == KC - 1))
                    mm.then_inc(mod_ready, 1)

            pe.wait_ge(silu_ready, 1)
            pe.wait_ge(dma_mod_first, 16)
            mod_rows(0)
            pe.wait_ge(dma_mod_rest, 16)
            mod_rows(1)
            mod_rows(2)
            pe.wait_ge(dma_const, 16 * 2)
            for g in range(2):
                pe.wait_ge(normed, GT * (ln_second(g) + 1))
                if g:
                    pe.wait_ge(mod_copied, 2)
                for k in range(KC):
                    for t in range(GT):
                        mm = pe.transpose(first_bank(4 + 2 * g + k)[:, t * P:(t + 1) * P], zs[g][:, t, k * P:(k + 1) * P], ident)
                    mm.then_inc(xt_ready, 1)

            def project(k, b, w, job):
                pe.wait_ge(x_out, 2 * (job - 1))
                project_into(pX, k, b, w).then_inc(x_job_ready, 1)

            def project_into(bank, k, b, w):
                for i in range(2):
                    t = 2 * k + i
                    for p, (s, m) in enumerate(PASSES):
                        for c in range(KC):
                            mm = pe.matmul(bank[:, i * D:(i + 1) * D], xT[b][:, s, c, t * P:(t + 1) * P], w[:, m, c, :],
                                           start=(p == 0 and c == 0), stop=(p == 2 and c == KC - 1))
                return mm

            def transpose_head(h, c, job):
                if not isinstance(job, int) or job > 1:
                    pe.wait_ge(x_out, 2 * (job - 1))
                for i in range(GT):
                    mm = pe.transpose(pX[:, i * P:(i + 1) * P], qn[:, GT * c + i, h, :], ident)
                mm.then_inc(x_job_ready, 1)

            pe.wait_ge(wkv_lo_ready, KC)
            pe.wait_ge(mod_copied, 6)
            for i in range(8):
                if i % 4 in (0, 2):
                    pe.wait_ge(xt_lo_ready, KC * (i % 4 // 2 + 1))
                if i == 4:
                    pe.wait_ge(wq_lo_ready, 1)
                    pe.wait_ge(xt_lo_ready, 2 * KC)
                project_into(first_bank(i), i % 4, 0, wkv_sb if i < 4 else wq_sb).then_inc(first_ready, 1)
            for i in range(4):
                pe.wait_ge(first_scaled, (4, 4, 6, 8)[i])
                pe.wait_ge(first_v_lo, 4)
                for t in range(GT):
                    block = GT * (i % 2) + t
                    mm = pe.transpose(first_bank(i)[:, t * P:(t + 1) * P], kn[:, block, :] if i < 2 else qn[:, block, 0, :], ident)
                mm.then_inc(first_t_ready, 1)

            def scores(b, s):
                h, j = (s // NT) % 2, s % NT
                for p, (a, m) in enumerate(PASSES):
                    for c in range(CH):
                        mm = pe.matmul(pS[:, s % 2, c, :], kT[b][:, a, j * P:(j + 1) * P], qT[:, h, m, c * BANK:(c + 1) * BANK],
                                       start=(p == 0), stop=(p == 2))
                mm.then_inc(scores_ready, 1)

            def weighted_values(it, b, s, fresh):
                j = s % NT
                pe.wait_ge(phi_ready, step(it, s) + 1)
                def part(p, a, m, c):
                    if m == LO:
                        pe.wait_ge(plo_ready, step(it, s) + 1)
                    moving = phi[:, s % 4, :] if m == HI else plo[:, s % 2, :]
                    return pe.matmul(pO[:, c, :], v[b][:, a, j, :], moving[:, c * BANK:(c + 1) * BANK],
                                     start=(j == 0 and p == 0), stop=(j == NT - 1 and p == 2))

                passes = list(enumerate(PASSES))
                if j:
                    for p, (a, m) in passes:
                        for c in range(CH):
                            mm = part(p, a, m, c)
                else:
                    for c in range(CH):
                        if not fresh:
                            pe.wait_ge(o_lo_ready, CH * (2 * it + s // NT - 1) + c + 1)
                        for p, (a, m) in passes:
                            mm = part(p, a, m, c)
                mm.then_inc(pv_done, 1)

            def sums(head, parity, c, free):
                pe.wait_ge(psum_added, 7 * (head + 1))
                if free:
                    pe.wait_ge(y_bank_free, y_job(head, c) - 1)
                for t in range(GT):
                    at = (GT * c + t) * P
                    mm = pe.transpose(pY[:, t * P:(t + 1) * P], psums[:, parity, at:at + P], ident)
                mm.then_inc(y_job_ready, 1)

            def project_out(head, k, parity, split):
                pe.wait_ge(y_bank_free, y_job(head, k + 1))
                if k == 0:
                    pe.wait_ge(o_lo_ready, CH * (head + 1))
                    pe.wait_ge(wout_lo_ready, split)
                for i in range(2):
                    t = 2 * k + i
                    for p, (a, m) in enumerate(PASSES):
                        mm = pe.matmul(pY[:, i * D:(i + 1) * D], oT[:, a, t * P:(t + 1) * P], wout_sb[:, parity, m, :], start=(p == 0), stop=(p == 2))
                mm.then_inc(y_job_ready, 1)

            pe.wait_ge(first_t_lo, 4)
            scores(0, 0)

            def between(slot):
                for g in range(GROUPS):
                    stage = stage_of(g, slot)
                    if stage in TRANSPOSES:
                        k = TRANSPOSES.index(stage)
                        pe.wait_ge(modulated, 2 * GROUPS + 4 * g + 4)
                        pe.wait_ge(x_out, 2 * (between_job(g, k) - 1))
                        for t in range(GT):
                            mm = pe.transpose(pX[:, t * P:(t + 1) * P], z[:, t, k * P:(k + 1) * P], ident)
                        mm.then_inc(x_job_ready, 1)
                    if stage == "logits":
                        pe.wait_ge(x_out, 2 * between_job(g, 1))
                        pe.wait_ge(router_lo, 1)
                        for p, (a, m) in enumerate(PASSES):
                            for c in range(KC):
                                mm = pe.matmul(pX[0:E, :], router_sb[:, a, c, :], xT[g // 2][:, m, c, (g % 2) * BANK:(g % 2 + 1) * BANK],
                                               start=(p == 0 and c == 0), stop=(p == 2 and c == KC - 1))
                        mm.then_inc(x_job_ready, 1)
                    if stage == "top_two":
                        pe.wait_ge(x_out, 2 * between_job(g, 2))
                        for t in range(GT):
                            mm = pe.transpose(pX[:, t * E:(t + 1) * E], logits_T[:, t * P:(t + 1) * P], ident[0:E, 0:E])
                        mm.then_inc(x_job_ready, 1)
                    if stage == "route_t":
                        pe.wait_ge(route_ready, g + 1)
                        pe.wait_ge(x_out, 2 * between_job(g, 3))
                        for t in range(GT):
                            mm = pe.transpose(pX[0:2 * E, t * P:(t + 1) * P], route[:, t, :], ident)
                        mm.then_inc(x_job_ready, 1)

            def up(n, parts=(0, 1)):
                g, t = n // RT, n % RT
                if n >= 2:
                    pe.wait_ge(u_done, n - 1)
                if g == 0:
                    pe.wait_ge(elo_ready, t + 1)
                if t == 0:
                    pe.wait_ge(x_out, 2 * between_job(g, 1))
                for u in parts:
                    for p, (a, m) in enumerate(PASSES):
                        for c in range(KC):
                            at = (KC * u + c) * P
                            mm = pe.matmul(pS[:, n % 2, u, :], expert_w[:, t, a, at:at + P],
                                           xT[g // 2][:, m, c, (g % 2) * BANK:(g % 2 + 1) * BANK],
                                           start=(p == 0 and c == 0), stop=(p == 2 and c == KC - 1))
                if parts[-1] == 1:
                    mm.then_inc(gu_ready, 1)

            def routing(n):
                g, t = n // RT, n % RT
                if t == 0:
                    pe.wait_ge(x_out, 2 * between_job(g, 4))
                if n:
                    pe.wait_ge(a_done, n)
                else:
                    pe.wait_ge(select_in, 16)
                    pe.wait_ge(y_bank_free, y_job(2 * ITERS - 1, 5))
                pe.matmul(pY[:, :], select[:, t * P:(t + 1) * P], rT[:, g % 2, :], start=True, stop=True).then_inc(cw_ready, 1)

            def down(n):
                g, t = n // RT, n % RT
                pe.wait_ge(alo_done, n + 1)
                if t == 0 and g:
                    pe.wait_ge(o_mul, g)
                for i in range(GT):
                    for p, (a, m) in enumerate(PASSES):
                        w = (act_hi, act_lo)[a][:, n % 2, i * P:(i + 1) * P]
                        mm = pe.matmul(pO[:, i // 2, (i % 2) * D:(i % 2 + 1) * D], w, expert_w[:, t, m, 2 * KC * P:TILE],
                                       start=(t == 0 and p == 0 and i % 2 == 0), stop=(t == RT - 1 and p == 2), skip_group_check=True)
                mm.then_inc(down_done, 1)

            def bank_x(it, b, jobs, name):
                k, job = int(name[-1]), x_job(it, b, jobs, name)
                q_batch = 1 if jobs is TURN else b
                if name[:-1] == "B":
                    transpose_head(1, k, job)
                if name[:-1] == "A":
                    pe.wait_ge(qn_ready, q_job(next_q(it, b, jobs), 2 * k + 1))
                    transpose_head(0, k, job)
                if name[:-1] == "KT":
                    pe.wait_ge(qn_ready, q_job(PAIRS - 1, 2 * k + 1))
                    transpose_head(0, k, job)
                if name[:-1] == "KV":
                    project(k, 1, wkv_sb, job)
                if name[:-1] == "Q":
                    if k == 0:
                        pe.wait_ge(wq_lo_ready, it + 2)
                    project(k, q_batch, wq_sb, job)
                if name[:-1] == "N":
                    pe.wait_ge(normed, GT * (ln_second(2 + it) + 1))
                    pe.wait_ge(x_out, 2 * (job - 1))
                    for t in range(GT):
                        mm = pe.transpose(pX[:, t * P:(t + 1) * P], z[:, t, k * P:(k + 1) * P], ident)
                    mm.then_inc(x_job_ready, 1)

            def steps(it, b, first, jobs):
                start, end = b == 0 and first, jobs is END
                for s in range(STEPS):
                    if not (end and s == STEPS - 1):
                        if not (start and s == 0):
                            pe.wait_ge(p32_ready, step(it, s))
                        if s == NT - 1:
                            pe.wait_ge(x_out, 2 * x_job(it, b, jobs, "B1"))
                        if s == STEPS - 1:
                            pe.wait_ge(x_out, 2 * x_job(it, b, jobs, "A1"))
                        scores(1 if jobs is TURN and s == STEPS - 1 else b, s + 1)
                    for name in jobs:
                        if jobs[name] == s:
                            bank_x(it, b, jobs, name)
                    if not start:
                        if s in ZB_AT:
                            sums(2 * it - 1, 1, ZB_AT.index(s), True)
                        if s in OB_AT:
                            project_out(2 * it - 1, OB_AT.index(s), 1, it)
                    if s in ZA_AT:
                        sums(2 * it, 0, ZA_AT.index(s), not start or s != ZA_AT[0])
                    if s in OA_AT:
                        project_out(2 * it, OA_AT.index(s), 0, it + 1)
                    if s:
                        weighted_values(it, b, s - 1, start and s == 1)
                    elif not start:
                        weighted_values(it - 1, b - 1 if first else b, STEPS - 1, False)
                    if first and b or end:
                        between(s if end else s - STEPS)

            iterations(pe, steps)
            weighted_values(ITERS - 1, B - 1, STEPS - 1, False)
            for c in range(CH):
                sums(2 * ITERS - 1, 1, c, True)
            for k in range(4):
                project_out(2 * ITERS - 1, k, 1, ITERS)
                if k == 0:
                    pe.wait_ge(p32_ready, STEPS * ITERS)
                up(k // 2, (k % 2,))
            routing(0)

            for n in range(GROUPS * RT):
                between(STEPS + n)
                if n + 2 < GROUPS * RT:
                    up(n + 2)
                if n + 1 < GROUPS * RT:
                    routing(n + 1)
                down(n)


LOOP = dict(B0=2, B1=3, Q0=4, Q1=6, Q2=7, Q3=10, A0=11, A1=13)
EARLY = dict(B0=2, B1=3, Q0=4, Q1=6, Q2=7, Q3=10, A0=11, A1=13, N0=14, N1=15)
TURN = dict(B0=0, B1=1, KV0=2, KV1=3, KV2=4, KV3=5, KT0=6, Q0=7, KT1=8, Q1=9, Q2=10, Q3=11, A0=12, A1=13)
END = dict(B0=0, B1=2)
Q_APPLY = dict(Q0=6, Q1=8, Q2=9, Q3=12)
APPLY = {len(LOOP): Q_APPLY, len(EARLY): Q_APPLY, len(END): {},
         len(TURN): dict(KV0=3, KV1=4, KV2=5, KV3=6, Q0=8, Q1=10, Q2=11, Q3=12)}
ENTRY = dict(stats_1=0, normalise_1=3, modulate_scale=4, modulate_shift=5, stats_2=6, normalise_2=10)
WQ_SPLIT, WOUT_SPLIT = 2, 9
ZB_AT, OB_AT = [1, 2], [3, 4, 5, 7]
ZA_AT, OA_AT = [9, 11], [12, 13, 14, 15]

TRANSPOSES = ("transpose_0", "transpose_1")
STAGES = ("stats_1", "normalise_1", "gate_multiply", "gate_add", "stats_2", "normalise_2", "modulate_scale",
          "modulate_shift", *TRANSPOSES, "logits", "top_two", "weights", "route_t")
BETWEEN = ((-9, -6, -5, -4, -2, 0, 2, 3, 5, 6, 8, 10, 13, 15),
           (5, 8, 9, 10, 12, 15, 17, 18, 19, 20, 21, 22, 24, 25),
           (19, 21, 22, 23, 24, 26, 27, 28, 29, 30, 31, 32, 34, 35),
           (29, 31, 32, 33, 34, 36, 37, 38, 39, 40, 41, 42, 44, 45))


def stage_of(g, slot):
    return STAGES[BETWEEN[g].index(slot)] if slot in BETWEEN[g] else None


AHEAD = 3


def head_pairs(wq):
    w = wq.reshape(KC, P, PAIRS, 2 * DH).transpose(2, 1, 0, 3).reshape(PAIRS, P, KC * 2 * DH)
    return np.concatenate([w, w[:1]])


def row_tiles(w1, w2):
    def stationary(w):
        return w.reshape(RT, P, KC, P).transpose(0, 3, 2, 1).reshape(RT, P, KC * P)
    down = w2.transpose(0, 2, 1).reshape(RT, P, D)
    return np.concatenate([stationary(w1[:, :INNER]), stationary(w1[:, INNER:]), down], axis=2)


def kernel(**inputs):
    import concourse.bacc as bacc
    from concourse.bass_utils import run_bass_kernel_spmd

    laid_out = {
        "x": np.asarray(inputs["L0_attn_x"]),
        "g_norm": np.asarray(inputs["L0_attn_g_norm"]).reshape(KC, P).T,
        "wq": head_pairs(np.asarray(inputs["L0_attn_Wq"])),
        "wkv": np.asarray(inputs["L0_attn_Wkv"]),
        "wout": np.asarray(inputs["L0_attn_Wout"]).reshape(PAIRS, 2, DH, D).transpose(0, 2, 1, 3).reshape(PAIRS, DH, 2 * D),
        "g_out": np.asarray(inputs["L0_attn_g_out"]),
        "router": np.asarray(inputs["L0_ffn_router_w"]).T,
        "experts_w": row_tiles(np.asarray(inputs["L0_ffn_w1"]), np.asarray(inputs["L0_ffn_w2"])),
        "cond": np.asarray(inputs["L0_c"]).T.reshape(KC, P, B).transpose(1, 0, 2),
        "wmod": np.asarray(inputs["L0_wmod"]),
        "consts": shape_constants(),
    }
    nc = bacc.Bacc("TRN2", target_bir_lowering=False, num_devices=1)
    arrays, args = {}, []
    for name, a in laid_out.items():
        a = np.ascontiguousarray(a)
        arrays[f"in_{name}"] = a
        args.append(nc.dram_tensor(f"in_{name}", a.shape, mybir.dt.from_np(a.dtype), kind="ExternalInput").ap())
    args.append(nc.dram_tensor("out_x", (B, N, D), F32, kind="ExternalOutput").ap())
    adaln_block(nc, *args)
    return run_bass_kernel_spmd(nc, [arrays], core_ids=[0]).results[0]["out_x"]
```
